# Optimizing a Trainium2 kernel written in Bass

```python
import numpy as np
import jax
import jax.numpy as jnp

def _softmax(x, axis=-1):
    return jax.nn.softmax(x, axis=axis)

def _gelu(x):
    return jax.nn.gelu(x, approximate=True)

def _silu(x):
    return jax.nn.silu(x)

def _sigmoid(x):
    return jax.nn.sigmoid(x)

def _layernorm(x, axis=-1, eps=1e-05):
    m = jnp.mean(x, axis=axis, keepdims=True)
    v = jnp.var(x, axis=axis, keepdims=True)
    return (x - m) / jnp.sqrt(v + eps)

def _scatter_add(tgt, idx, src, axis=0):
    return tgt.at[idx].add(src)

def _segment_sum(src, seg, n):
    return jax.ops.segment_sum(src, seg, n)
kernel_name = 'mk_sandwich_d1_jaxref_r4_17c95f'

def setup_inputs(seed: int=0):
    np.random.seed(seed)
    _w = jnp.asarray

    def _L0_attn_setup():
        import jax, jax.numpy as jnp
        import numpy as np
        HID = 256
        RATIO = 4
        SELECT_K = 128
        WINDOW = 64
        N_HEADS = 16
        SCALE = 1.0 / np.sqrt(HID // N_HEADS)

        def _adjust(t, L):
            cur = t.shape[1]
            if cur < L:
                return jnp.pad(t, ((0, 0), (0, L - cur), (0, 0)))
            return t[:, :L]

        def _attend(x, Wq, bq, Wk, bk, Wv, bv):
            q = x @ Wq + bq
            k = x @ Wk + bk
            v = x @ Wv + bv
            s = jnp.einsum('...qd,...kd->...qk', q, k) * SCALE
            p = jax.nn.softmax(s, axis=-1)
            return jnp.einsum('...qk,...kd->...qd', p, v)
        key = jax.random.key(seed)
        ks = jax.random.split(key, 12)
        std = 0.02
        d = {'hidden_states': jax.random.normal(ks[0], (4, 1024, HID), jnp.float32), 'Wq': jax.random.normal(ks[1], (HID, HID), jnp.float32) * std, 'bq': jnp.zeros((HID,), jnp.float32), 'Wk': jax.random.normal(ks[2], (HID, HID), jnp.float32) * std, 'bk': jnp.zeros((HID,), jnp.float32), 'Wv': jax.random.normal(ks[3], (HID, HID), jnp.float32) * std, 'bv': jnp.zeros((HID,), jnp.float32), 'Wo': jax.random.normal(ks[4], (3 * HID, HID), jnp.float32) * std, 'bo': jnp.zeros((HID,), jnp.float32), 'Wg': jax.random.normal(ks[5], (HID, 3), jnp.float32) * std, 'bg': jnp.zeros((3,), jnp.float32), 'Wc': jax.random.normal(ks[6], (RATIO * HID, HID), jnp.float32) * std, 'bc': jnp.zeros((HID,), jnp.float32), 'Ws': jax.random.normal(ks[7], (HID, 1), jnp.float32) * std, 'bs': jnp.zeros((1,), jnp.float32)}
        return d
    _L0_attn_in = _L0_attn_setup()

    def _L0_ffn_setup():
        import jax, jax.numpy as jnp
        import numpy as np
        DIM = 256
        DEPTH = 2
        HEADS = 8
        DIM_HEAD = 64
        WINDOW = 128
        INNER = HEADS * DIM_HEAD
        HID = int(DIM * 4 * 2 / 3)
        B, N = (2, 2048)
        QK_SCALE = 8.0

        def shift_token(t):
            t1, t2 = jnp.split(t, 2, axis=-1)
            t2 = jnp.pad(t2, ((0, 0), (1, 0), (0, 0)))[:, :-1]
            return jnp.concatenate([t1, t2], axis=-1)

        def l2norm(t):
            return t / jnp.clip(jnp.linalg.norm(t, axis=-1, keepdims=True), 1e-12)

        def rotate_half(x):
            x1, x2 = jnp.split(x, 2, axis=-1)
            return jnp.concatenate([-x2, x1], axis=-1)

        def rotary_xpos(q, k):
            n = q.shape[-2]
            half_idx = jnp.arange(0, DIM_HEAD, 2, dtype=jnp.float32)
            inv_freq = 1.0 / 10000.0 ** (half_idx / DIM_HEAD)
            t = jnp.arange(n, dtype=jnp.float32)
            freqs = t[:, None] * inv_freq[None, :]
            freqs = jnp.concatenate([freqs, freqs], axis=-1)
            base = (half_idx + 0.4 * DIM_HEAD) / (1.4 * DIM_HEAD)
            power = (t - n // 2) / float(WINDOW // 2)
            scale = base[None, :] ** power[:, None]
            scale = jnp.concatenate([scale, scale], axis=-1)
            cos, sin = (jnp.cos(freqs), jnp.sin(freqs))
            q = q * cos * scale + rotate_half(q) * sin * scale
            k = k * cos / scale + rotate_half(k) * sin / scale
            return (q, k)

        def local_attention(q, k, v):
            b, h, n, d = q.shape
            w = n // WINDOW
            bq = q.reshape(b, h, w, WINDOW, d) * QK_SCALE
            bk = k.reshape(b, h, w, WINDOW, d)
            bv = v.reshape(b, h, w, WINDOW, d)

            def look_around(t):
                p = jnp.pad(t, ((0, 0), (0, 0), (1, 0), (0, 0), (0, 0)))
                return jnp.concatenate([p[:, :, :w], p[:, :, 1:]], axis=3)
            bk, bv = (look_around(bk), look_around(bv))
            bt = jnp.arange(n).reshape(w, WINDOW)
            btp = jnp.pad(bt, ((1, 0), (0, 0)), constant_values=-1)
            btk = jnp.concatenate([btp[:w], btp[1:]], axis=1)
            sim = jnp.einsum('bhwid,bhwjd->bhwij', bq, bk)
            i = bt[:, :, None]
            j = btk[:, None, :]
            mask = (i < j) | (i > j + WINDOW) | (j == -1)
            sim = jnp.where(mask, -jnp.finfo(sim.dtype).max, sim)
            attn = jax.nn.softmax(sim, axis=-1)
            out = jnp.einsum('bhwij,bhwjd->bhwid', attn, bv)
            return out.reshape(b, h, n, d)

        def _layer(x, wqkv, qs, ksc, wo, lg, lb, w1, b1, w2, b2):
            b, n, _ = x.shape
            h = shift_token(x)
            qkv = h @ wqkv
            q, k, v = jnp.split(qkv, 3, axis=-1)
            to_heads = lambda t: t.reshape(b, n, HEADS, DIM_HEAD).transpose(0, 2, 1, 3)
            q, k, v = (to_heads(q), to_heads(k), to_heads(v))
            q = l2norm(q) * qs
            k = l2norm(k) * ksc
            q, k = rotary_xpos(q, k)
            o = local_attention(q, k, v)
            o = o.transpose(0, 2, 1, 3).reshape(b, n, INNER)
            x = x + o @ wo
            h = shift_token(x)
            mu = h.mean(-1, keepdims=True)
            var = h.var(-1, keepdims=True)
            h = (h - mu) / jnp.sqrt(var + 1e-05) * lg + lb
            h = h @ w1 + b1
            a, g = jnp.split(h, 2, axis=-1)
            h = a * jax.nn.gelu(g, approximate=False)
            x = x + h @ w2 + b2
            return x
        key = jax.random.key(seed)
        ks = jax.random.split(key, 6)
        return {'x': jax.random.normal(ks[0], (B, N, DIM), jnp.float32), 'wqkv': jax.random.normal(ks[1], (DEPTH, DIM, 3 * INNER), jnp.float32) * 0.02, 'q_scale': jnp.ones((DEPTH, DIM_HEAD), jnp.float32), 'k_scale': jnp.ones((DEPTH, DIM_HEAD), jnp.float32), 'wo': jax.random.normal(ks[2], (DEPTH, INNER, DIM), jnp.float32) * 0.02, 'ln_g': jnp.ones((DEPTH, DIM), jnp.float32), 'ln_b': jnp.zeros((DEPTH, DIM), jnp.float32), 'w1': jax.random.normal(ks[3], (DEPTH, DIM, 2 * HID), jnp.float32) * 0.02, 'b1': jnp.zeros((DEPTH, 2 * HID), jnp.float32), 'w2': jax.random.normal(ks[4], (DEPTH, HID, DIM), jnp.float32) * 0.02, 'b2': jnp.zeros((DEPTH, DIM), jnp.float32)}
    _L0_ffn_in = _L0_ffn_setup()
    _d = {'L0_attn_hidden_states': _L0_attn_in['hidden_states'], 'L0_attn_Wq': _L0_attn_in['Wq'], 'L0_attn_bq': _L0_attn_in['bq'], 'L0_attn_Wk': _L0_attn_in['Wk'], 'L0_attn_bk': _L0_attn_in['bk'], 'L0_attn_Wv': _L0_attn_in['Wv'], 'L0_attn_bv': _L0_attn_in['bv'], 'L0_attn_Wo': _L0_attn_in['Wo'], 'L0_attn_bo': _L0_attn_in['bo'], 'L0_attn_Wg': _L0_attn_in['Wg'], 'L0_attn_bg': _L0_attn_in['bg'], 'L0_attn_Wc': _L0_attn_in['Wc'], 'L0_attn_bc': _L0_attn_in['bc'], 'L0_attn_Ws': _L0_attn_in['Ws'], 'L0_attn_bs': _L0_attn_in['bs'], 'L0_ffn_wqkv': _L0_ffn_in['wqkv'], 'L0_ffn_q_scale': _L0_ffn_in['q_scale'], 'L0_ffn_k_scale': _L0_ffn_in['k_scale'], 'L0_ffn_wo': _L0_ffn_in['wo'], 'L0_ffn_ln_g': _L0_ffn_in['ln_g'], 'L0_ffn_ln_b': _L0_ffn_in['ln_b'], 'L0_ffn_w1': _L0_ffn_in['w1'], 'L0_ffn_b1': _L0_ffn_in['b1'], 'L0_ffn_w2': _L0_ffn_in['w2'], 'L0_ffn_b2': _L0_ffn_in['b2']}
    _x0 = _d['L0_attn_hidden_states']
    _d['L0_attn_hidden_states'] = jax.random.normal(jax.random.fold_in(jax.random.key(seed), 1), (2, 2048, 256), dtype=_x0.dtype)
    del _x0
    return _d

def reference(L0_attn_hidden_states, L0_attn_Wq, L0_attn_bq, L0_attn_Wk, L0_attn_bk, L0_attn_Wv, L0_attn_bv, L0_attn_Wo, L0_attn_bo, L0_attn_Wg, L0_attn_bg, L0_attn_Wc, L0_attn_bc, L0_attn_Ws, L0_attn_bs, L0_ffn_wqkv, L0_ffn_q_scale, L0_ffn_k_scale, L0_ffn_wo, L0_ffn_ln_g, L0_ffn_ln_b, L0_ffn_w1, L0_ffn_b1, L0_ffn_w2, L0_ffn_b2):

    def _L0_attn_ref(hidden_states, Wq, bq, Wk, bk, Wv, bv, Wo, bo, Wg, bg, Wc, bc, Ws, bs):
        import jax, jax.numpy as jnp
        import numpy as np
        HID = 256
        RATIO = 4
        SELECT_K = 128
        WINDOW = 64
        N_HEADS = 16
        SCALE = 1.0 / np.sqrt(HID // N_HEADS)

        def _adjust(t, L):
            cur = t.shape[1]
            if cur < L:
                return jnp.pad(t, ((0, 0), (0, L - cur), (0, 0)))
            return t[:, :L]

        def _attend(x, Wq, bq, Wk, bk, Wv, bv):
            q = x @ Wq + bq
            k = x @ Wk + bk
            v = x @ Wv + bv
            s = jnp.einsum('...qd,...kd->...qk', q, k) * SCALE
            p = jax.nn.softmax(s, axis=-1)
            return jnp.einsum('...qk,...kd->...qd', p, v)
        B, L, H = hidden_states.shape
        gates = jax.nn.sigmoid(hidden_states @ Wg + bg)
        gates = gates / (gates.sum(-1, keepdims=True) + 1e-06)
        pad_c = -L % RATIO
        xc = jnp.pad(hidden_states, ((0, 0), (0, pad_c), (0, 0)))
        blocks = xc.reshape(B, -1, RATIO * H)
        compressed = blocks @ Wc + bc
        comp_out = _adjust(_attend(compressed, Wq, bq, Wk, bk, Wv, bv), L)
        k_eff = min(SELECT_K, L)
        scores = (hidden_states @ Ws + bs)[..., 0]
        _, idx = jax.lax.top_k(scores, k_eff)
        idx = jnp.sort(idx, axis=-1)
        selected = jnp.take_along_axis(hidden_states, idx[..., None], axis=1)
        sel_out = _adjust(_attend(selected, Wq, bq, Wk, bk, Wv, bv), L)
        W = min(WINDOW, L)
        pad_w = -L % W
        xw = jnp.pad(hidden_states, ((0, 0), (0, pad_w), (0, 0)))
        Lp = xw.shape[1]
        starts = np.arange(0, Lp - W + 1, W // 2)
        widx = starts[:, None] + np.arange(W)
        win = xw[:, widx]
        win_ctx = _attend(win, Wq, bq, Wk, bk, Wv, bv)
        win_out = _adjust(win_ctx.reshape(B, -1, H), L)
        combined = jnp.concatenate([comp_out * gates[..., 0:1], sel_out * gates[..., 1:2], win_out * gates[..., 2:3]], axis=-1)
        out = combined @ Wo + bo
        out = out * 0.5 + hidden_states * 0.5
        mu = out.mean(-1, keepdims=True)
        var = out.var(-1, keepdims=True)
        return (out - mu) * jax.lax.rsqrt(var + 1e-06)

    def _L0_ffn_ref(x, wqkv, q_scale, k_scale, wo, ln_g, ln_b, w1, b1, w2, b2):
        import jax, jax.numpy as jnp
        import numpy as np
        DIM = 256
        DEPTH = 2
        HEADS = 8
        DIM_HEAD = 64
        WINDOW = 128
        INNER = HEADS * DIM_HEAD
        HID = int(DIM * 4 * 2 / 3)
        B, N = (2, 2048)
        QK_SCALE = 8.0

        def shift_token(t):
            t1, t2 = jnp.split(t, 2, axis=-1)
            t2 = jnp.pad(t2, ((0, 0), (1, 0), (0, 0)))[:, :-1]
            return jnp.concatenate([t1, t2], axis=-1)

        def l2norm(t):
            return t / jnp.clip(jnp.linalg.norm(t, axis=-1, keepdims=True), 1e-12)

        def rotate_half(x):
            x1, x2 = jnp.split(x, 2, axis=-1)
            return jnp.concatenate([-x2, x1], axis=-1)

        def rotary_xpos(q, k):
            n = q.shape[-2]
            half_idx = jnp.arange(0, DIM_HEAD, 2, dtype=jnp.float32)
            inv_freq = 1.0 / 10000.0 ** (half_idx / DIM_HEAD)
            t = jnp.arange(n, dtype=jnp.float32)
            freqs = t[:, None] * inv_freq[None, :]
            freqs = jnp.concatenate([freqs, freqs], axis=-1)
            base = (half_idx + 0.4 * DIM_HEAD) / (1.4 * DIM_HEAD)
            power = (t - n // 2) / float(WINDOW // 2)
            scale = base[None, :] ** power[:, None]
            scale = jnp.concatenate([scale, scale], axis=-1)
            cos, sin = (jnp.cos(freqs), jnp.sin(freqs))
            q = q * cos * scale + rotate_half(q) * sin * scale
            k = k * cos / scale + rotate_half(k) * sin / scale
            return (q, k)

        def local_attention(q, k, v):
            b, h, n, d = q.shape
            w = n // WINDOW
            bq = q.reshape(b, h, w, WINDOW, d) * QK_SCALE
            bk = k.reshape(b, h, w, WINDOW, d)
            bv = v.reshape(b, h, w, WINDOW, d)

            def look_around(t):
                p = jnp.pad(t, ((0, 0), (0, 0), (1, 0), (0, 0), (0, 0)))
                return jnp.concatenate([p[:, :, :w], p[:, :, 1:]], axis=3)
            bk, bv = (look_around(bk), look_around(bv))
            bt = jnp.arange(n).reshape(w, WINDOW)
            btp = jnp.pad(bt, ((1, 0), (0, 0)), constant_values=-1)
            btk = jnp.concatenate([btp[:w], btp[1:]], axis=1)
            sim = jnp.einsum('bhwid,bhwjd->bhwij', bq, bk)
            i = bt[:, :, None]
            j = btk[:, None, :]
            mask = (i < j) | (i > j + WINDOW) | (j == -1)
            sim = jnp.where(mask, -jnp.finfo(sim.dtype).max, sim)
            attn = jax.nn.softmax(sim, axis=-1)
            out = jnp.einsum('bhwij,bhwjd->bhwid', attn, bv)
            return out.reshape(b, h, n, d)

        def _layer(x, wqkv, qs, ksc, wo, lg, lb, w1, b1, w2, b2):
            b, n, _ = x.shape
            h = shift_token(x)
            qkv = h @ wqkv
            q, k, v = jnp.split(qkv, 3, axis=-1)
            to_heads = lambda t: t.reshape(b, n, HEADS, DIM_HEAD).transpose(0, 2, 1, 3)
            q, k, v = (to_heads(q), to_heads(k), to_heads(v))
            q = l2norm(q) * qs
            k = l2norm(k) * ksc
            q, k = rotary_xpos(q, k)
            o = local_attention(q, k, v)
            o = o.transpose(0, 2, 1, 3).reshape(b, n, INNER)
            x = x + o @ wo
            h = shift_token(x)
            mu = h.mean(-1, keepdims=True)
            var = h.var(-1, keepdims=True)
            h = (h - mu) / jnp.sqrt(var + 1e-05) * lg + lb
            h = h @ w1 + b1
            a, g = jnp.split(h, 2, axis=-1)
            h = a * jax.nn.gelu(g, approximate=False)
            x = x + h @ w2 + b2
            return x
        for l in range(DEPTH):
            x = _layer(x, wqkv[l], q_scale[l], k_scale[l], wo[l], ln_g[l], ln_b[l], w1[l], b1[l], w2[l], b2[l])
        return x
    x = L0_attn_hidden_states
    x = x + _layernorm(_L0_attn_ref(_layernorm(x, axis=-1), L0_attn_Wq, L0_attn_bq, L0_attn_Wk, L0_attn_bk, L0_attn_Wv, L0_attn_bv, L0_attn_Wo, L0_attn_bo, L0_attn_Wg, L0_attn_bg, L0_attn_Wc, L0_attn_bc, L0_attn_Ws, L0_attn_bs), axis=-1)
    x = x + _layernorm(_L0_ffn_ref(_layernorm(x, axis=-1), L0_ffn_wqkv, L0_ffn_q_scale, L0_ffn_k_scale, L0_ffn_wo, L0_ffn_ln_g, L0_ffn_ln_b, L0_ffn_w1, L0_ffn_b1, L0_ffn_w2, L0_ffn_b2), axis=-1)
    return x

_drawn_inputs = setup_inputs


def setup_inputs(seed=0):
    import zlib

    import numpy as np

    out = dict(_drawn_inputs(seed))
    spreads = {'L0_attn_bq': (0.0, 0.8),
     'L0_attn_bk': (0.0, 2.0),
     'L0_attn_bv': (0.0, 0.8),
     'L0_attn_bo': (0.0, 0.1),
     'L0_attn_bg': (0.0, 0.8),
     'L0_attn_bc': (0.0, 0.8),
     'L0_ffn_q_scale': (1.0, 0.6),
     'L0_ffn_k_scale': (1.0, 0.6),
     'L0_ffn_ln_g': (1.0, 0.6),
     'L0_ffn_ln_b': (0.0, 0.8),
     'L0_ffn_b1': (0.0, 0.8),
     'L0_ffn_b2': (0.0, 0.433)}
    factors = {'L0_attn_Wq': 8.0,
     'L0_attn_Wk': 8.0,
     'L0_attn_Wv': 8.0,
     'L0_attn_Wo': 8.0,
     'L0_attn_Wg': 8.0,
     'L0_attn_Wc': 8.0,
     'L0_attn_Ws': 8.0,
     'L0_ffn_wqkv': 5.348,
     'L0_ffn_wo': 5.108,
     'L0_ffn_w1': 3.487,
     'L0_ffn_w2': 3.476}
    for name, (base, spread) in spreads.items():
        noise = np.random.default_rng([zlib.crc32(name.encode()), seed]).standard_normal(out[name].shape)
        drawn = base * np.exp(spread * noise) if base else spread * noise
        out[name] = jnp.asarray(drawn.astype(out[name].dtype))
    for name, factor in factors.items():
        out[name] = (out[name] * factor).astype(out[name].dtype)
    return out
```

```python
from contextlib import ExitStack

import numpy as np

import concourse.bass as bass
from concourse import mybir

ALU = mybir.AluOpType
ACT = mybir.ActivationFunctionType
F32 = mybir.dt.float32
F32R = mybir.dt.float32r
AX_X = mybir.AxisListType.X

P = 128
B, N, D = 2, 2048, 256
DC = D // P
NB = B * N // P
BPB = N // P
GB = 4
NG = NB // GB
GPB = NG // B
GT = GB * P

RATIO, SEL, WIN = 4, 128, 64
NCOMP = N // RATIO
SCALE = 0.25
WK = WIN + WIN // 2
ROUNDS = SEL // 8

DEPTH, HEADS, DH = 2, 8, 64
INNER = HEADS * DH
QK_SCALE = 8.0
HID = 682
FC = 6
FW = 114
BIG = 1e30
MARK = -3.4e38


def fw(j):
    return min(FW, HID - j * FW)


def hs_slot(t):
    return t + t // BPB


def build(nc, x0, Wq, bq, Wk, bk, Wv, bv, Wo, bo, Wg, bg, Wc, bc, Ws, bs,
          wqkv, q_scale, k_scale, wo, ln_g, ln_b, w1, b1, w2, b2, rope_base, out):
    with ExitStack() as ctx:
        base = [(nc.sbuf_base + 63) // 64 * 64]

        def place(name, shape, dt=F32):
            size = 4 * int(np.prod(shape[1:]))
            at = base[0]
            base[0] += (size + 31) // 32 * 32
            assert base[0] <= nc.sbuf_top, (name, base[0])
            return nc.alloc_sbuf_tensor_at(name, shape, dt, offset=at)

        def sem(name):
            return ctx.enter_context(nc.semaphore(name))

        x_sb = place("x_sb", [P, NB, D])
        hs_attn = place("hs_attn", [P, NB + B, P])
        hs_ffn = place("hs_ffn", [P, NB + B, P])
        ident = place("ident", [P, P])
        mask_tab = place("mask_tab", [P, 2, P])
        mask_odd = place("mask_odd", [P, 2, P])
        mask_even = place("mask_even", [P, 2, P])
        neg_half = place("neg_half", [P, 16])
        warm = place("warm", [P, 1])
        raw = place("raw", [P, 3, 1536])
        stage0_base = base[0]

        rope_at = base[0]
        rope = place("rope", [P, BPB, 2, 2, DH])
        wqkv_hi = place("wqkv_hi", [P, DC, 3 * INNER], F32R)
        wqkv_lo = place("wqkv_lo", [P, DC, 3 * INNER], F32R)
        wo_sb = place("wo_sb", [P, INNER // P, D])
        w1_hi = place("w1_hi", [P, DC, 2 * HID], F32R)
        w1_lo = place("w1_lo", [P, DC, 2 * HID], F32R)
        w2_hi = place("w2_hi", [P, FC, D], F32R)
        w2_lo = place("w2_lo", [P, FC, D], F32R)
        qk_sc = place("qk_sc", [P, 2, DH])
        sc_x = place("sc_x", [P, 2, 2, DH])
        ln_gb = place("ln_gb", [P, 2, DC])
        b1_sb = place("b1_sb", [P, 2, FC])
        b2_sb = place("b2_sb", [P, D])
        work_base = base[0]
        h_in = place("h_in", [P, DC, P])
        hT_hi = place("hT_hi", [P, DC, P], F32R)
        hT_lo = place("hT_lo", [P, DC, P], F32R)
        qk_cos = place("qk_cos", [P, 2, INNER])
        qk_sin = place("qk_sin", [P, 2, INNER])
        qk_sq = place("qk_sq", [P, 2, INNER])
        sumsq = place("sumsq", [P, 2 * HEADS])
        rnorm = place("rnorm", [P, 2 * HEADS])
        qT = place("qT", [P, HEADS // 2, 2, P])
        kT = place("kT", [P, HEADS // 2, 2, P])
        v_sb = place("v_sb", [P, 2, INNER])
        prob = place("prob", [P, 6, 2, P])
        neg_max = place("neg_max", [P, HEADS])
        psums = place("psums", [P, HEADS])
        pinv = place("pinv", [P, HEADS])
        pT = place("pT", [P, 2, 4 * P])
        oT = place("oT", [P, INNER // P, P])
        base[0] = rope_at
        hn = place("hn", [P, GB, D])
        h_full = place("h_full", [P, DC, GT])
        gelu_sb = place("gelu_sb", [P, 2, GT])
        act_full = place("act_full", [P, 2, GT])
        base[0] = work_base
        h_hi = place("h_hi", [P, 2, DC, GT], F32R)
        h_lo = place("h_lo", [P, 2, DC, GT], F32R)
        act_hi = place("act_hi", [P, 3, GT], F32R)
        act_lo = place("act_lo", [P, 3, GT], F32R)
        bst = place("bst", [P, GB, 2, 6])
        mv = place("mv", [P, GB, 2])
        rstd = place("rstd", [P, GB])
        base[0] = work_base
        f_x1 = place("f_x1", [P, 2, GB, D])
        f_y = place("f_y", [P, 2, GB, D])
        f_bst = place("f_bst", [P, GB, 6])
        f_mv = place("f_mv", [P, 2, GB, 2])
        f_rstd = place("f_rstd", [P, 2, GB])

        base[0] = stage0_base
        xnT = place("xnT", [P, DC, B * N])
        wq_sb = place("wq_sb", [P, DC, D])
        wk_sb = place("wk_sb", [P, DC, D])
        wv_sb = place("wv_sb", [P, DC, D])
        wc_sb = place("wc_sb", [P, RATIO * DC, D])
        wo3_sb = place("wo3_sb", [P, 3 * DC, D])
        wsg_sb = place("wsg_sb", [P, DC, 36])
        bsg_sb = place("bsg_sb", [P, 1])
        bqkc_sb = place("bqkc_sb", [P, 3, DC])
        bv_bc = place("bv_bc", [P, D])
        bo_bc = place("bo_bc", [P, D])
        rows = place("rows", [64, N])
        left = place("left", [64, N])
        place_row = place("place_row", [64, N])
        top8 = place("top8", [64, 8])
        iota1 = place("iota1", [P, P])
        turned = raw[:, 2, 0:BPB * 64].rearrange("p (c n) -> p c n", n=64)
        gate = place("gate", [P, BPB, B, 3])
        gsum = place("gsum", [P, BPB, B])
        mask_win = place("mask_win", [P, WK])
        after_const = base[0]
        x_in = place("x_in", [P, 2, GB, D])
        xn_st = place("xn_st", [P, GB, D])
        l_bst = place("l_bst", [P, GB, 6])
        l_mv = place("l_mv", [P, GB, 2])
        l_rstd = place("l_rstd", [P, GB])
        l_t = place("l_t", [P, 6, GB])
        base[0] = after_const
        xw = place("xw", [P, DC, WK])
        qTw = place("qTw", [P, DC, 2, WIN])
        kTw = place("kTw", [P, DC, WK])
        vw = place("vw", [P, D])
        pw = place("pw", [P, WK])
        w_max = place("w_max", [P, 4])
        pTw = place("pTw", [P, P])
        cTw = place("cTw", [P, DC, P])
        base[0] = after_const
        tokT = place("tokT", [P, DC, NCOMP])
        qTc = place("qTc", [P, DC, NCOMP])
        kTc = place("kTc", [P, DC, NCOMP])
        vc = place("vc", [P, NCOMP // P, D])
        pc = place("pc", [P, NCOMP])
        pTc = place("pTc", [P, NCOMP // P, NCOMP])
        c_max = place("c_max", [P, 4])
        sel_m = place("sel_m", [P, 2, P])
        cT = place("cT", [P, DC, B * NCOMP + B * P])

        bank = ctx.enter_context(nc.psum_tensor("bank", [P, 8, 512], F32))
        x1_dram = nc.dram_tensor("x1_scratch", [NB, P, D], F32, kind="Internal").ap()

        consts_ready = sem("consts_ready")
        phase_done = sem("phase_done")
        waited = sem("waited")

        def settle(eng):
            eng.sem_inc(waited, 1)

        def end_phase(eng, n):
            eng.drain().then_inc(phase_done, 1)
            eng.wait_ge(phase_done, 5 * n)
            settle(eng)

        w_loaded = sem("w_loaded")
        w_small = sem("w_small")
        x_loaded = [sem("x_loaded0"), sem("x_loaded1")]
        l_stats = sem("l_stats")
        l_stat_step = sem("l_stat_step")
        l_eps = sem("l_eps")
        l_rs = sem("l_rs")
        l_norm = sem("l_norm")
        l_step = sem("l_step")
        l_norm2 = sem("l_norm2")
        l_x1 = sem("l_x1")
        l_xf = sem("l_xf")
        xnT_ps = sem("xnT_ps")
        xnT_ready = sem("xnT_ready")
        rows_zero = sem("rows_zero")
        rows_ps = sem("rows_ps")
        rows_ready = sem("rows_ready")
        x1_stored = sem("x1_stored")
        hs_moved = sem("hs_moved")
        row_t_ps = sem("row_t_ps")
        row_t_ready = sem("row_t_ready")
        gate_step = sem("gate_step")
        gate_exp = sem("gate_exp")
        gates_ready = sem("gates_ready")
        win_x = sem("win_x")
        win_q_ps = sem("win_q_ps")
        win_k_ps = sem("win_k_ps")
        win_v_ps = sem("win_v_ps")
        win_q = sem("win_q")
        win_k = sem("win_k")
        win_v = sem("win_v")
        win_s = sem("win_s")
        win_m = sem("win_m")
        win_nm = sem("win_nm")
        win_e = sem("win_e")
        win_f = sem("win_f")
        win_p = sem("win_p")
        win_pt_ps = sem("win_pt_ps")
        win_pt = sem("win_pt")
        win_c_ps = sem("win_c_ps")
        win_c = sem("win_c")
        win_o = sem("win_o")
        win_add = sem("win_add")
        topk_step = sem("topk_step")
        pos_ps = sem("pos_ps")
        pos_ready = sem("pos_ready")
        tok_ps = sem("tok_ps")
        tok_ready = sem("tok_ready")
        com_qk_ps = sem("com_qk_ps")
        com_qk = sem("com_qk")
        com_v_ps = sem("com_v_ps")
        com_v = sem("com_v")
        com_s = sem("com_s")
        com_m = sem("com_m")
        com_nm = sem("com_nm")
        com_e = sem("com_e")
        com_f = sem("com_f")
        com_p = sem("com_p")
        com_pt_ps = sem("com_pt_ps")
        com_pt = sem("com_pt")
        com_c_ps = sem("com_c_ps")
        com_c = sem("com_c")
        sel_made = sem("sel_made")
        sel_used = sem("sel_used")
        com_o = sem("com_o")
        com_add = sem("com_add")
        bo_added = sem("bo_added")
        raw_attn = sem("raw_attn")
        raw_ffn = sem("raw_ffn")
        split_hi = sem("split_hi")
        split_lo = sem("split_lo")
        wo_loaded = sem("wo_loaded")
        sc_made = sem("sc_made")
        rope_made = sem("rope_made")
        kv_zero = sem("kv_zero")
        h_staged = sem("h_staged")
        mask_set = sem("mask_set")
        hT_ps = sem("hT_ps")
        hT_hi_ready = sem("hT_hi_ready")
        hT_lo_ready = sem("hT_lo_ready")
        qk_raw = sem("qk_raw")
        v_raw = sem("v_raw")
        squares = sem("squares")
        rotated = sem("rotated")
        ss_ready = sem("ss_ready")
        ss_floor = sem("ss_floor")
        r_ready = sem("r_ready")
        zk_ready = sem("zk_ready")
        zq_ready = sem("zq_ready")
        qk_ready = sem("qk_ready")
        kT_ps = sem("kT_ps")
        qT_ps = sem("qT_ps")
        kT_ready = sem("kT_ready")
        q_even = sem("q_even")
        q_odd = sem("q_odd")
        v_ready = sem("v_ready")
        s_ready = sem("s_ready")
        masked = sem("masked")
        exped = sem("exped")
        inverted = sem("inverted")
        p_even = sem("p_even")
        p_odd = sem("p_odd")
        pt_ps = sem("pt_ps")
        pt_ready = sem("pt_ready")
        pv_done = sem("pv_done")
        ot_ready = sem("ot_ready")
        wo_ps = sem("wo_ps")
        x_attn = sem("x_attn")
        hs_ffn_moved = sem("hs_ffn_moved")
        n_stats = sem("n_stats")
        n_aggr = sem("n_aggr")
        n_eps = sem("n_eps")
        n_rs = sem("n_rs")
        n_norm = sem("n_norm")
        nT_ps = sem("nT_ps")
        nT_hi = sem("nT_hi")
        nT_full = sem("nT_full")
        nT_lo = sem("nT_lo")
        g_ps = sem("g_ps")
        a_ps = sem("a_ps")
        g_ready = sem("g_ready")
        act_ready = sem("act_ready")
        act_hi_ready = sem("act_hi_ready")
        act_lo_ready = sem("act_lo_ready")
        w2_used = sem("w2_used")
        acc_ps = sem("acc_ps")
        b2_added = sem("b2_added")
        x_ffn = sem("x_ffn")
        hs_attn_moved = sem("hs_attn_moved")
        small_loaded = sem("small_loaded")
        f_x1_loaded = [sem("f_x1_loaded0"), sem("f_x1_loaded1")]
        f_stats = sem("f_stats")
        f_step = sem("f_step")
        f_eps = sem("f_eps")
        f_rs = sem("f_rs")
        f_norm = sem("f_norm")
        f_sum = sem("f_sum")
        out_stored = [sem("out_stored0"), sem("out_stored1")]

        x0_b = x0.rearrange("b (t p) d -> (b t) p d", p=P)
        out_b = out.rearrange("b (t p) d -> (b t) p d", p=P)

        def group_of(dram, g):
            return dram[bass.ds(g * GB, GB), :, :].rearrange("t p d -> p t d")

        def col(v):
            return v.rearrange("(c p) -> p c", p=P)

        def row_bc(v):
            return v.rearrange("(o n) -> o n", o=1).broadcast_to([P, v.shape[0]])

        NLOAD = 10
        JOBS = [(NCOMP, 0, 0, 0), (NCOMP, 1, NCOMP, 4), (P, 0, B * NCOMP, 8), (P, 1, B * NCOMP + P, 9)]
        ctx.enter_context(nc.allow_non_contiguous_dma(reason="biases and scales, a few hundred elements"))
        block = ctx.enter_context(nc.Block())

        @block.sync
        def _(sp):
            for g in range(2):
                sp.dma_start(x_in[:, g], group_of(x0_b, g)).then_inc(x_loaded[g], 16)
            sp.wait_ge(rows_zero, 2)
            for b in range(B):
                sp.dma_start(wsg_sb[:, :, 32 * b:32 * b + 1], Ws.rearrange("(c p) n -> p c n", p=P)).then_inc(w_small, 16)
                sp.dma_start(wsg_sb[:, :, 32 * b + 1:32 * b + 4], Wg.rearrange("(c p) n -> p c n", p=P)).then_inc(w_small, 16)
                sp.dma_start(bsg_sb[32 * b:32 * b + 1, :], bs.rearrange("(p o) -> p o", o=1)).then_inc(w_small, 16)
                sp.dma_start(bsg_sb[32 * b + 1:32 * b + 4, :], bg.rearrange("(p o) -> p o", o=1)).then_inc(w_small, 16)
            for w_sb, w in ((wq_sb, Wq), (wk_sb, Wk), (wv_sb, Wv)):
                sp.dma_start(w_sb[:], w.rearrange("(c p) n -> p c n", p=P)).then_inc(w_loaded, 16)
            sp.dma_start(wo3_sb[:], Wo.rearrange("(c p) n -> p c n", p=P)).then_inc(w_loaded, 16)
            sp.dma_start(wc_sb[:], Wc.rearrange("(c p) n -> p c n", p=P)).then_inc(w_loaded, 16)
            for i, v in enumerate((bq, bk, bc)):
                sp.dma_start(bqkc_sb[:, i], col(v)).then_inc(w_loaded, 16)
            sp.dma_start(bv_bc[:], row_bc(bv)).then_inc(w_loaded, 16)
            sp.dma_start(bo_bc[:], row_bc(bo)).then_inc(w_loaded, 16)
            with sp.Fori(0, NG // 2 - 1) as u:
                for i in range(2):
                    sp.wait_ge(l_norm, u * (2 * GB) + (i + 1) * GB)
                    sp.dma_start(x_in[:, i], group_of(x0_b, u * 2 + 2 + i)).then_inc(x_loaded[i], 16)
            sp.dma_start(raw[:, 0:2], wqkv[0].rearrange("(c p) n -> p c n", p=P)).then_inc(raw_attn, 16)
            end_phase(sp, 1)
            end_phase(sp, 2)
            end_phase(sp, 3)
            for i in range(2):
                sp.dma_start(x_in[:, i], group_of(x0_b, i)).then_inc(x_loaded[i], 16)
            with sp.Fori(0, NG // 2) as u:
                for i in range(2):
                    g = u * 2 + i
                    sp.wait_ge(l_xf, (g + 1) * GB)
                    sp.dma_start(group_of(x1_dram, g), x_in[:, i]).then_inc(x1_stored, 16)
                    sp.dma_start(hs_attn[1:P, bass.ds(g * GB + g // GPB, GB), :],
                                 x_sb[0:P - 1, bass.ds(g * GB, GB), P:D]).then_inc(hs_moved, 16)
                    sp.dma_start(hs_attn[0:1, bass.ds(g * GB + g // GPB + 1, GB), :],
                                 x_sb[P - 1:P, bass.ds(g * GB, GB), P:D]).then_inc(hs_moved, 16)
                    sp.wait_ge(x1_stored, 16 * (g + 1))
                    sp.dma_start(x_in[:, i], group_of(x0_b, (g + 2) % NG)).then_inc(x_loaded[i], 16)
            sp.wait_ge(hs_moved, 32 * NG)
            for i in range(2):
                sp.wait_ge(x_loaded[i], 16 * (NG + 1))
            end_phase(sp, 4)

            with sp.Fori(0, DEPTH) as lay:
                sp.dma_start(qk_sc[:, 0], q_scale[lay].rearrange("(o n) -> o n", o=1).broadcast_to([P, DH])).then_inc(small_loaded, 16)
                sp.dma_start(qk_sc[:, 1], k_scale[lay].rearrange("(o n) -> o n", o=1).broadcast_to([P, DH])).then_inc(small_loaded, 16)
                sp.dma_start(raw[:, 2, 0:BPB * 64], rope_base[:, 0]).then_inc(small_loaded, 16)
                sp.dma_start(rope[:, :, 0, 0, :], rope_base[:, 1].rearrange("p (t d) -> p t d", t=BPB)).then_inc(small_loaded, 16)
                sp.dma_start(wo_sb[:], wo[lay].rearrange("(c p) n -> p c n", p=P)).then_inc(wo_loaded, 16)
                sp.dma_start(ln_gb[:, 0], col(ln_g[lay])).then_inc(wo_loaded, 16)
                sp.dma_start(ln_gb[:, 1], col(ln_b[lay])).then_inc(wo_loaded, 16)
                for i in range(2):
                    sp.dma_start(b1_sb[0:FW, i, 0:FC - 1], b1[lay][i * HID:i * HID + (FC - 1) * FW].rearrange("(c p) -> p c", p=FW)).then_inc(wo_loaded, 16)
                    sp.dma_start(b1_sb[0:fw(FC - 1), i, FC - 1:FC], b1[lay][i * HID + (FC - 1) * FW:(i + 1) * HID].rearrange("(c p) -> p c", c=1)).then_inc(wo_loaded, 16)
                sp.dma_start(b2_sb[:], b2[lay].rearrange("(o n) -> o n", o=1).broadcast_to([P, D])).then_inc(wo_loaded, 16)
                end_phase(sp, 5 + 4 * lay)
                sp.dma_start(raw[:, 0:2, 0:2 * HID], w1[lay].rearrange("(c p) n -> p c n", p=P)).then_inc(raw_ffn, 16)
                raw_w2 = raw[:, 2, :].rearrange("p (c n) -> p c n", n=D)
                sp.dma_start(raw_w2[0:FW, 0:FC - 1], w2[lay][0:(FC - 1) * FW, :].rearrange("(c p) n -> p c n", p=FW)).then_inc(raw_ffn, 16)
                sp.dma_start(raw_w2[0:fw(FC - 1), FC - 1], w2[lay][(FC - 1) * FW:HID, :]).then_inc(raw_ffn, 16)
                with sp.Fori(0, NB) as t:
                    sp.wait_ge(x_attn, lay * NB + t + 1)
                    sp.dma_start(hs_ffn[1:P, t + t // BPB, :], x_sb[0:P - 1, t, P:D]).then_inc(hs_ffn_moved, 16)
                    sp.dma_start(hs_ffn[0:1, t + t // BPB + 1, :], x_sb[P - 1:P, t, P:D]).then_inc(hs_ffn_moved, 16)
                sp.wait_ge(hs_ffn_moved, 32 * NB * (lay + 1))
                settle(sp)
                sp.wait_ge(raw_ffn, 48 * (lay + 1))
                settle(sp)
                end_phase(sp, 6 + 4 * lay)
                end_phase(sp, 7 + 4 * lay)
                sp.dma_start(raw[:, 0:2], wqkv[(lay + 1) % DEPTH].rearrange("(c p) n -> p c n", p=P)).then_inc(raw_attn, 16)
                with sp.Fori(0, NG) as g:
                    sp.wait_ge(x_ffn, (lay * NG + g + 1) * 2)
                    sp.dma_start(hs_attn[1:P, bass.ds(g * GB + g // GPB, GB), :],
                                 x_sb[0:P - 1, bass.ds(g * GB, GB), P:D]).then_inc(hs_attn_moved, 16)
                    sp.dma_start(hs_attn[0:1, bass.ds(g * GB + g // GPB + 1, GB), :],
                                 x_sb[P - 1:P, bass.ds(g * GB, GB), P:D]).then_inc(hs_attn_moved, 16)
                sp.wait_ge(hs_attn_moved, 32 * NG * (lay + 1))
                settle(sp)
                sp.wait_ge(raw_attn, 16 * (lay + 2))
                settle(sp)
                end_phase(sp, 8 + 4 * lay)

            for i in range(2):
                sp.dma_start(f_x1[:, i], group_of(x1_dram, i)).then_inc(f_x1_loaded[i], 16)
            with sp.Fori(0, NG // 2) as u:
                for i in range(2):
                    g = u * 2 + i
                    sp.wait_ge(f_sum, g + 1)
                    sp.dma_start(group_of(out_b, g), f_y[:, i]).then_inc(out_stored[i], 16)
                    sp.dma_start(f_x1[:, i], group_of(x1_dram, (g + 2) % NG)).then_inc(f_x1_loaded[i], 16)
            for i in range(2):
                sp.wait_ge(out_stored[i], 16 * (NG // 2))
                sp.wait_ge(f_x1_loaded[i], 16 * (NG // 2 + 1))

        @block.gpsimd
        def _(pool):
            step = [0]
            pool.memset(ident[:], 0.0).then_inc(sc_made, 1)
            pool.memset(mask_tab[:, 0], BIG).then_inc(sc_made, 1)
            pool.memset(mask_tab[:, 1], 0.0).then_inc(sc_made, 1)
            pool.memset(mask_even[:], 0.0).then_inc(sc_made, 1)
            pool.memset(mask_win[:], 0.0).then_inc(sc_made, 1)
            pool.memset(neg_half[:], -0.5).then_inc(sc_made, 1)
            pool.memset(hs_attn[:], 0.0).then_inc(sc_made, 1)
            pool.memset(hs_ffn[:], 0.0).then_inc(sc_made, 1)
            pool.memset(rows[:], 0.0).then_inc(rows_zero, 1)
            pool.memset(wsg_sb[:], 0.0).then_inc(rows_zero, 1)
            pool.memset(warm[:], 1.0).then_inc(sc_made, 1)
            pool.iota(iota1[:], pattern=[[1, P]], base=1, channel_multiplier=0,
                      allow_small_or_imprecise_dtypes=True).then_inc(sc_made, 1)
            pool.wait_ge(sc_made, 10)
            pool.affine_select(out=ident[:], in_=ident[:], compare_op=ALU.not_equal, fill=1.0, base=0,
                               pattern=[[-1, P]], channel_multiplier=1).then_inc(sc_made, 1)
            pool.affine_select(out=mask_tab[:, 1], in_=mask_tab[:, 1], compare_op=ALU.is_ge, fill=BIG, base=0,
                               pattern=[[1, P]], channel_multiplier=-1).then_inc(sc_made, 1)
            pool.affine_select(out=mask_even[:, 0], in_=mask_even[:, 0], compare_op=ALU.is_ge, fill=BIG, base=0,
                               pattern=[[-1, P]], channel_multiplier=1).then_inc(sc_made, 1)
            pool.wait_ge(sc_made, 13)
            pool.affine_select(out=mask_win[0:WIN], in_=mask_win[0:WIN], compare_op=ALU.is_gt, fill=-BIG, base=WIN,
                               pattern=[[-1, WK]], channel_multiplier=0).then_inc(sc_made, 1)
            pool.wait_ge(sc_made, 14)
            pool.affine_select(out=mask_win[WIN:P], in_=mask_win[WIN:P], compare_op=ALU.is_ge, fill=-BIG, base=-WIN // 2,
                               pattern=[[1, WK]], channel_multiplier=0).then_inc(sc_made, 1)
            pool.wait_ge(sc_made, 15)
            pool.tensor_copy(mask_odd[:, 0], mask_tab[:, 1]).then_inc(sc_made, 1)
            pool.tensor_copy(mask_odd[:, 1], mask_even[:, 0]).then_inc(sc_made, 1)
            pool.wait_ge(sc_made, 17)
            pool.tensor_copy(mask_even[:, 1], mask_tab[:, 1]).then_inc(consts_ready, 1)

            def inverse_root(var, out_ap, eps, ready, n_ready, stepped, n_step, done, width):
                pool.wait_ge(ready, n_ready)
                settle(pool)
                pool.tensor_scalar(out_ap, var, eps, None, ALU.add).then_inc(stepped, 1)
                pool.wait_ge(stepped, n_step)
                settle(pool)
                pool.tensor_tensor(out_ap, out_ap, neg_half[:, 0:width], ALU.pow).then_inc(done, 1)

            with pool.Fori(0, NG) as g:
                inverse_root(l_mv[:, :, 1], l_rstd[:], 1e-5, l_stats, (g + 1) * GB, l_eps, g + 1, l_rs, GB)
            end_phase(pool, 1)
            end_phase(pool, 2)
            with pool.Fori(0, NB) as j:
                pool.tensor_tensor(x_sb[:, j, :], x_sb[:, j, :], bo_bc[:], ALU.add).then_inc(bo_added, 1)
            end_phase(pool, 3)
            with pool.Fori(0, NG) as g:
                inverse_root(l_t[:, 0], l_t[:, 1], 1e-6, l_step, NG + 4 * g + 1, l_eps, 3 * g + NG + 1, l_rs, GB)
                inverse_root(l_t[:, 2], l_t[:, 3], 1e-5, l_step, NG + 4 * g + 3, l_eps, 3 * g + NG + 2, l_rs, GB)
                inverse_root(l_mv[:, :, 1], l_rstd[:], 1e-5, l_norm2, (g + 1) * 3 * GB, l_eps, 3 * g + NG + 3, l_rs, GB)
            end_phase(pool, 4)

            with pool.Fori(0, DEPTH) as lay:
                pool.wait_ge(small_loaded, 64 * (lay + 1))
                settle(pool)
                pool.tensor_scalar(sc_x[:, 0, 0], qk_sc[:, 0], -QK_SCALE, None, ALU.mult).then_inc(sc_made, 1)
                pool.tensor_copy(sc_x[:, 0, 1], qk_sc[:, 1]).then_inc(sc_made, 1)
                for i, s in ((0, QK_SCALE), (1, -1.0)):
                    pool.tensor_scalar(sc_x[:, 1, i, 0:32], qk_sc[:, i, 32:64], s, None, ALU.mult).then_inc(sc_made, 1)
                    pool.tensor_scalar(sc_x[:, 1, i, 32:64], qk_sc[:, i, 0:32], -s, None, ALU.mult).then_inc(sc_made, 1)
                pool.wait_ge(sc_made, 17 + 6 * (lay + 1))
                cs = raw[:, 2, 0:BPB * 64].rearrange("p (t k d) -> p t k d", t=BPB, k=2)
                sn = rope[:, :, 0, 0, :].rearrange("p t (k d) -> p t k d", k=2)
                for i in range(2):
                    for h in range(2):
                        pool.tensor_tensor(rope[:, :, 1, i, 32 * h:32 * h + 32], sn[:, :, i, :],
                                           sc_x[:, 1, i, 32 * h:32 * h + 32][:, None, :].broadcast_to([P, BPB, 32]),
                                           ALU.mult).then_inc(rope_made, 1)
                pool.wait_ge(rope_made, 8 * lay + 4)
                for i in range(2):
                    for h in range(2):
                        pool.tensor_tensor(rope[:, :, 0, i, 32 * h:32 * h + 32], cs[:, :, i, :],
                                           sc_x[:, 0, i, 32 * h:32 * h + 32][:, None, :].broadcast_to([P, BPB, 32]),
                                           ALU.mult).then_inc(rope_made, 1)
                end_phase(pool, 5 + 4 * lay)

                def stage_h(t):
                    pool.tensor_copy(h_in[:, 0], x_sb[:, t, 0:P]).then_inc(h_staged, 1)
                    pool.tensor_copy(h_in[:, 1], hs_attn[:, t + t // BPB, :]).then_inc(h_staged, 1)

                def front(f):
                    pool.wait_ge(ss_floor, f + 1)
                    settle(pool)
                    pool.tensor_tensor(rnorm[:], sumsq[:], neg_half[:], ALU.pow).then_inc(r_ready, 1)
                    pool.wait_ge(rotated, 3 * f + 3)
                    pool.tensor_tensor(qk_cos[:, 0], qk_cos[:, 0], qk_sin[:, 0], ALU.add).then_inc(zq_ready, 1)

                f0 = lay * (NB + 1)
                stage_h(0)
                pool.tensor_copy(mask_even[:, 1], mask_tab[:, 0]).then_inc(mask_set, 1)
                front(f0)
                for t in (1, 2):
                    pool.wait_ge(hT_ps, f0 + lay + t)
                    settle(pool)
                    stage_h(t)
                with pool.Fori(0, NB // 2) as u:
                    for i in range(2):
                        t = u * 2 + i
                        if i == 0:
                            pool.wait_ge(masked, (lay * NB + t + 1) * HEADS + 2 * lay)
                            settle(pool)
                            pool.tensor_copy(mask_even[:, 1], mask_tab[:, ((u + 1) % (BPB // 2) + (BPB // 2 - 1)) // (BPB // 2)]).then_inc(mask_set, 1)
                        front(f0 + t + 1)
                        pool.wait_ge(hT_ps, f0 + lay + t + 3)
                        pool.wait_ge(x_attn, lay * NB + t)
                        settle(pool)
                        stage_h((t + 3) % NB)
                end_phase(pool, 6 + 4 * lay)

                end_phase(pool, 7 + 4 * lay)

                def norm_lo(n, half):
                    for c in range(DC):
                        pool.wait_ge(nT_full, 2 * n + c + 1)
                        pool.wait_ge(nT_hi, 2 * n + c + 1)
                        settle(pool)
                        pool.tensor_tensor(h_lo[:, half, c], h_full[:, c], h_hi[:, half, c], ALU.subtract).then_inc(nT_lo, 1)

                n0 = lay * (NG + 1)
                inverse_root(mv[:, :, 1], rstd[:], 1e-5, n_aggr, (n0 + 1) * GB, n_eps, n0 + 1, n_rs, GB)
                norm_lo(n0, 0)
                with pool.Fori(0, NG // 2) as u:
                    for i in range(2):
                        g = u * 2 + i
                        k = lay * NG + g
                        pool.wait_ge(n_norm, 8 * (n0 + g + 1))
                        settle(pool)
                        pool.tensor_tensor(x_sb[:, bass.ds(g * GB, GB), :], x_sb[:, bass.ds(g * GB, GB), :],
                                           b2_sb[:, None, :].broadcast_to([P, GB, D]), ALU.add).then_inc(b2_added, 1)
                        for j in range(FC):
                            if j == 1:
                                inverse_root(mv[:, :, 1], rstd[:], 1e-5, n_aggr, (n0 + g + 2) * GB, n_eps, n0 + g + 2, n_rs, GB)
                            pool.wait_ge(act_hi_ready, FC * k + j + 1)
                            if j >= 3:
                                pool.wait_ge(w2_used, FC * k + j - 2)
                            settle(pool)
                            w = fw(j)
                            pool.tensor_tensor(act_lo[0:w, j % 3], act_full[0:w, j % 2], act_hi[0:w, j % 3], ALU.subtract).then_inc(act_lo_ready, 1)
                        norm_lo(n0 + g + 1, 1 - i)
                end_phase(pool, 8 + 4 * lay)

            with pool.Fori(0, NG // 2) as u:
                for i in range(2):
                    g = u * 2 + i
                    inverse_root(f_mv[:, i, :, 1], f_rstd[:, i], 1e-5, f_stats, (g + 1) * GB, f_eps, g + 1, f_rs, GB)

        @block.scalar
        def _(act):
            act.wait_ge(consts_ready, 1)
            act.activation(warm[:], warm[:], ACT.Exp).then_inc(gate_exp, 1)
            for b in range(B):
                with act.Fori(0, GPB) as gg:
                    g = gg + b * GPB
                    for c in range(DC):
                        act.wait_ge(xnT_ps, 2 * g + c + 1)
                        settle(act)
                        act.activation(xnT[:, c, bass.ds(g * GT, GT)], bank[:, c], ACT.Copy).then_inc(xnT_ready, 1)
                    act.wait_ge(rows_zero, 2)
                    act.wait_ge(w_small, 16 * 8)
                    act.wait_ge(rows_ps, g + 1)
                    settle(act)
                    act.activation(rows[32 * b:32 * b + 4, bass.ds(gg * GT, GT)], bank[32 * b:32 * b + 4, 2],
                                   ACT.Identity, bias=bsg_sb[32 * b:32 * b + 4, :]).then_inc(rows_ready, 1)
            end_phase(act, 1)

            act.wait_ge(row_t_ready, 1)
            act.activation(gate[:, :, 0], turned[:, :, 1:4], ACT.Exp, scale=-1.0).then_inc(gate_exp, 1)
            act.activation(gate[:, :, 1], turned[:, :, 33:36], ACT.Exp, scale=-1.0).then_inc(gate_exp, 1)
            act.wait_ge(w_loaded, 16 * NLOAD)
            for job, (T, b, at, n0) in enumerate(JOBS):
                act.wait_ge(tok_ps, job + 1)
                for m in range(DC):
                    if T == NCOMP:
                        act.activation(tokT[:, m, 0:T], bank[:, m, 0:T], ACT.Identity, bias=bqkc_sb[:, 2, m:m + 1]).then_inc(tok_ready, 1)
                    else:
                        act.activation(tokT[:, m, 0:T], bank[:, m, 0:T], ACT.Copy).then_inc(tok_ready, 1)
                for i, dst in enumerate((qTc, kTc)):
                    for m in range(DC):
                        act.wait_ge(com_qk_ps, 4 * job + 2 * i + m + 1)
                        act.activation(dst[:, m, 0:T], bank[:, 2 + 2 * i + m, 0:T], ACT.Identity, bias=bqkc_sb[:, i, m:m + 1]).then_inc(com_qk, 1)
                for qb in range(T // P):
                    act.wait_ge(com_nm, n0 + qb + 1)
                    act.activation(pc[:, 0:T], bank[:, 6, 0:T], ACT.Exp, bias=c_max[:, 1:2], scale=SCALE, accum_out=c_max[:, 2:3]).then_inc(com_e, 1)
                    act.wait_ge(com_pt_ps, n0 + qb + 1)
                    act.activation(pTc[:, 0:T // P, qb * P:(qb + 1) * P], bank[:, 7, 0:T].rearrange("p (k q) -> p k q", q=P), ACT.Copy).then_inc(com_pt, 1)
                act.wait_ge(com_c_ps, job + 1)
                act.activation(cT[:, :, at:at + T], bank[:, 0:2, 0:T], ACT.Copy).then_inc(com_c, 1)
            end_phase(act, 2)

            def win_front(j, tok):
                act.wait_ge(win_v_ps, j)
                settle(act)
                act.activation(xw[:], xnT[:, :, bass.ds(tok, WK)], ACT.Copy).then_inc(win_x, 1)

            def win_qk(j):
                act.wait_ge(win_q_ps, j + 1)
                act.wait_ge(win_s, j)
                for m in range(DC):
                    for w in range(2):
                        act.activation(qTw[:, m, w, :], bank[:, 0, m * WK + w * WIN // 2:m * WK + w * WIN // 2 + WIN],
                                       ACT.Identity, bias=bqkc_sb[:, 0, m:m + 1]).then_inc(win_q, 1)
                act.wait_ge(win_k_ps, j + 1)
                for m in range(DC):
                    act.activation(kTw[:, m], bank[:, 1, m * WK:(m + 1) * WK],
                                   ACT.Identity, bias=bqkc_sb[:, 1, m:m + 1]).then_inc(win_k, 1)

            win_front(0, 0)
            win_qk(0)
            with act.Fori(0, NB) as j:
                jn = (j + 1) % NB
                win_front(j + 1, (jn // BPB) * N + (jn % BPB) * WIN)
                act.wait_ge(win_nm, j + 1)
                act.activation(pw[:], pw[:], ACT.Exp, bias=w_max[:, 1:2], scale=SCALE,
                               accum_out=w_max[:, 2:3]).then_inc(win_e, 1)
                win_qk(j + 1)
                act.wait_ge(win_pt_ps, j + 1)
                act.activation(pTw[0:WK, :], bank[0:WK, 4, 0:P], ACT.Copy).then_inc(win_pt, 1)
                act.wait_ge(win_c_ps, j + 1)
                act.activation(cTw[:], bank[:, 5, 0:2 * P].rearrange("p (m q) -> p m q", m=DC), ACT.Copy).then_inc(win_c, 1)
            end_phase(act, 3)
            end_phase(act, 4)

            with act.Fori(0, DEPTH) as lay:
                act.activation(warm[:], warm[:], ACT.Exp).then_inc(gate_exp, 1)
                act.wait_ge(raw_attn, 16 * (lay + 1))
                for c in range(DC):
                    act.activation(wqkv_hi[:, c], raw[:, c], ACT.Copy).then_inc(split_hi, 1)
                end_phase(act, 5 + 4 * lay)

                def hi(g):
                    act.wait_ge(hT_ps, g + 1)
                    act.activation(hT_hi[:], bank[:, 5, 0:2 * P].rearrange("p (c t) -> p c t", c=DC), ACT.Copy).then_inc(hT_hi_ready, 1)

                def square(f):
                    act.wait_ge(qk_raw, f + 1)
                    act.activation(qk_sq[:], bank[:, 0:2], ACT.Square).then_inc(squares, 1)

                def q_out(f):
                    act.wait_ge(qT_ps, f + 1)
                    act.activation(qT[DH:P, :, 1, :], bank[DH:P, 0].rearrange("p (c t) -> p c t", t=P), ACT.Copy).then_inc(q_odd, 1)

                def v_out(f, half):
                    act.wait_ge(v_raw, f + 1)
                    act.activation(v_sb[:, half], bank[:, 2], ACT.Copy).then_inc(v_ready, 1)

                def exponent(k, h):
                    act.wait_ge(masked, HEADS * k + 2 * lay + h + 1)
                    act.activation(prob[:, h % 6], prob[:, h % 6], ACT.Exp, bias=neg_max[:, h:h + 1], scale=-1.0,
                                   accum_out=psums[:, h:h + 1]).then_inc(exped, 1)

                def weigh_odd(k, h):
                    act.wait_ge(inverted, HEADS * k + h + 1)
                    act.activation(prob[:, h % 6], prob[:, h % 6], ACT.Copy, scale=pinv[:, h:h + 1]).then_inc(p_odd, 1)

                def probs_out(k, j):
                    act.wait_ge(pt_ps, 4 * k + j + 1)
                    if j >= 2:
                        act.wait_ge(pv_done, 4 * k + j - 1)
                    act.activation(pT[:, j % 2], bank[:, 5 + j % 2], ACT.Copy).then_inc(pt_ready, 1)

                f0 = lay * (NB + 1)
                hi(f0 + lay)
                square(f0)
                v_out(f0, 0)
                hi(f0 + lay + 1)
                act.wait_ge(kv_zero, 3 * lay + 3)
                q_out(f0)
                with act.Fori(0, NB // 2) as u:
                    for i in range(2):
                        k = lay * NB + u * 2 + i
                        f = f0 + u * 2 + i + 1
                        for h in range(4):
                            exponent(k, h)
                        weigh_odd(k, 1)
                        exponent(k, 4)
                        exponent(k, 5)
                        weigh_odd(k, 3)
                        square(f)
                        probs_out(k, 0)
                        exponent(k, 6)
                        exponent(k, 7)
                        weigh_odd(k, 5)
                        probs_out(k, 1)
                        weigh_odd(k, 7)
                        probs_out(k, 2)
                        probs_out(k, 3)
                        hi(f + lay + 1)
                        act.wait_ge(pv_done, 4 * k + 4)
                        act.activation(oT[:], bank[:, 7].rearrange("p (c t) -> p c t", t=P), ACT.Copy).then_inc(ot_ready, 1)
                        v_out(f, 1 - i)
                        q_out(f)
                end_phase(act, 6 + 4 * lay)

                act.activation(warm[:], warm[:], ACT.Gelu).then_inc(gate_exp, 1)
                act.wait_ge(raw_ffn, 48 * (lay + 1))
                for c in range(DC):
                    act.activation(w1_hi[:, c], raw[:, c, 0:2 * HID], ACT.Copy).then_inc(split_hi, 1)
                raw_w2 = raw[:, 2, :].rearrange("p (c n) -> p c n", n=D)
                act.activation(w2_hi[0:FW, 0:FC - 1], raw_w2[0:FW, 0:FC - 1], ACT.Copy).then_inc(split_hi, 1)
                act.activation(w2_hi[0:fw(FC - 1), FC - 1], raw_w2[0:fw(FC - 1), FC - 1], ACT.Copy).then_inc(split_hi, 1)
                end_phase(act, 7 + 4 * lay)

                def norm_hi(n, half):
                    for c in range(DC):
                        act.wait_ge(nT_ps, n + 1)
                        act.activation(h_hi[:, half, c], bank[:, 6 + c], ACT.Identity, bias=ln_gb[:, 1, c:c + 1],
                                       scale=ln_gb[:, 0, c:c + 1]).then_inc(nT_hi, 1)

                n0 = lay * (NG + 1)
                act.wait_ge(wo_loaded, 16 * 8 * (lay + 1))
                norm_hi(n0, 0)
                with act.Fori(0, NG // 2) as u:
                    for i in range(2):
                        k = lay * NG + u * 2 + i
                        for j in range(FC):
                            w = fw(j)
                            act.wait_ge(g_ps, FC * k + j + 1)
                            if j >= 2:
                                act.wait_ge(act_ready, FC * k + j - 1)
                            act.activation(gelu_sb[0:w, j % 2], bank[0:w, j % 2], ACT.Gelu, bias=b1_sb[0:w, 1, j:j + 1]).then_inc(g_ready, 1)
                            if j == 4:
                                norm_hi(n0 + u * 2 + i + 1, 1 - i)
                end_phase(act, 8 + 4 * lay)

        @block.tensor
        def _(pe):
            pe.wait_ge(consts_ready, 1)
            pe.wait_ge(w_small, 16 * 8)
            for b in range(B):
                with pe.Fori(0, GPB) as gg:
                    g = gg + b * GPB
                    pe.wait_ge(l_norm, (g + 1) * GB)
                    for c in range(DC):
                        if c == 0:
                            pe.wait_ge(xnT_ready, 2 * g)
                        for i in range(GB):
                            tr = pe.transpose(bank[:, c, i * P:(i + 1) * P], xn_st[:, i, c * P:(c + 1) * P], ident[:])
                        tr.then_inc(xnT_ps, 1)
                    pe.wait_ge(xnT_ready, 2 * g + 2)
                    pe.wait_ge(rows_ready, g)
                    for c in range(DC):
                        mm = pe.matmul(bank[0:36, 2], wsg_sb[:, c], xnT[:, c, bass.ds(g * GT, GT)],
                                       start=(c == 0), stop=(c == DC - 1))
                    mm.then_inc(rows_ps, 1)
            end_phase(pe, 1)

            for c in range(BPB):
                tr = pe.transpose(bank[:, 6 + c // 8, (c % 8) * 64:(c % 8) * 64 + 64], rows[:, c * P:(c + 1) * P], ident[0:64, 0:64])
            tr.then_inc(row_t_ps, 1)

            pe.wait_ge(w_loaded, 16 * NLOAD)

            def attend(job, T, at, n0):
                pe.wait_ge(tok_ready, 2 * (job + 1))
                for i, w_sb in enumerate((wq_sb, wk_sb)):
                    for m in range(DC):
                        for c in range(DC):
                            mm = pe.matmul(bank[:, 2 + 2 * i + m, 0:T], w_sb[:, c, m * P:(m + 1) * P], tokT[:, c, 0:T], start=(c == 0), stop=(c == DC - 1))
                        mm.then_inc(com_qk_ps, 1)
                for kb in range(T // P):
                    for c in range(DC):
                        mm = pe.matmul(bank[:, kb // 2, (kb % 2) * D:(kb % 2 + 1) * D], tokT[:, c, kb * P:(kb + 1) * P], wv_sb[:, c],
                                       start=(c == 0), stop=(c == DC - 1))
                mm.then_inc(com_v_ps, 1)
                pe.wait_ge(com_qk, 4 * (job + 1))
                for qb in range(T // P):
                    n = n0 + qb
                    pe.wait_ge(com_e, n)
                    for c in range(DC):
                        mm = pe.matmul(bank[:, 6, 0:T], qTc[:, c, qb * P:(qb + 1) * P], kTc[:, c, 0:T], start=(c == 0), stop=(c == DC - 1))
                    mm.then_inc(com_s, 1)
                    pe.wait_ge(com_p, n + 1)
                    pe.wait_ge(com_pt, n)
                    for kb in range(T // P):
                        tr = pe.transpose(bank[:, 7, kb * P:(kb + 1) * P], pc[:, kb * P:(kb + 1) * P], ident[:])
                    tr.then_inc(com_pt_ps, 1)
                pe.wait_ge(com_v, job + 1)
                pe.wait_ge(com_pt, n0 + T // P)
                for m in range(DC):
                    for kb in range(T // P):
                        mm = pe.matmul(bank[:, m, 0:T], vc[:, kb, m * P:(m + 1) * P], pTc[:, kb, 0:T], start=(kb == 0), stop=(kb == T // P - 1))
                mm.then_inc(com_c_ps, 1)

            for job, (T, b, at, n0) in enumerate(JOBS):
                if job:
                    pe.wait_ge(com_c, job)
                if T == NCOMP:
                    for m in range(DC):
                        n = 0
                        for r in range(RATIO):
                            for c in range(DC):
                                xr = xnT[:, c, b * N:(b + 1) * N].rearrange("p (i r) -> p r i", r=RATIO)[:, r]
                                mm = pe.matmul(bank[:, m], wc_sb[:, r * DC + c, m * P:(m + 1) * P], xr, start=(n == 0), stop=(n == RATIO * DC - 1))
                                n += 1
                    mm.then_inc(tok_ps, 1)
                else:
                    if b == 0:
                        pe.wait_ge(topk_step, 2 * ROUNDS + 4)
                        pe.wait_ge(com_e, n0)
                        pe.wait_ge(com_pt, n0)
                        for c in range(BPB):
                            tr = pe.transpose(bank[:, 6 + c // 8, (c % 8) * 64:(c % 8) * 64 + 64], place_row[:, c * P:(c + 1) * P], ident[0:64, 0:64])
                        tr.then_inc(pos_ps, 1)
                    for c in range(BPB):
                        n = b * BPB + c
                        pe.wait_ge(sel_made, n + 1)
                        for m in range(DC):
                            mm = pe.matmul(bank[:, m, 0:P], x_sb[:, n, m * P:(m + 1) * P], sel_m[:, n % 2], start=(c == 0), stop=(c == BPB - 1))
                        mm.then_inc(sel_used, 1)
                    pe.drain().then_inc(tok_ps, 1)
                    if b == 0:
                        pe.wait_ge(pos_ready, 1)
                attend(job, T, at, n0)
            pe.wait_ge(com_c, len(JOBS))
            for n in range(B * (NCOMP // P)):
                b, qb = divmod(n, NCOMP // P)
                if n:
                    pe.wait_ge(com_add, n)
                terms = [(cT[:, m, n * P:(n + 1) * P], m) for m in range(DC)]
                if qb == 0:
                    at = B * NCOMP + b * P
                    terms += [(cT[:, m, at:at + P], DC + m) for m in range(DC)]
                for i, (c_ap, row) in enumerate(terms):
                    mm = pe.matmul(bank[:, 6, 0:D], c_ap, wo3_sb[:, row], start=(i == 0), stop=(i == len(terms) - 1))
                mm.then_inc(com_o, 1)
            end_phase(pe, 2)

            def win_qkv(j):
                pe.wait_ge(win_x, j + 1)
                for i, w_sb in enumerate((wq_sb, wk_sb)):
                    for m in range(DC):
                        for c in range(DC):
                            mm = pe.matmul(bank[:, i, m * WK:(m + 1) * WK], w_sb[:, c, m * P:(m + 1) * P], xw[:, c], start=(c == 0), stop=(c == DC - 1))
                    mm.then_inc((win_q_ps, win_k_ps)[i], 1)
                pe.wait_ge(win_v, j)
                for c in range(DC):
                    mm = pe.matmul(bank[0:WK, 2, 0:D], xw[:, c], wv_sb[:, c], start=(c == 0), stop=(c == DC - 1))
                mm.then_inc(win_v_ps, 1)

            win_qkv(0)
            with pe.Fori(0, NB) as j:
                pe.wait_ge(win_q, 4 * j + 4)
                pe.wait_ge(win_k, 2 * j + 2)
                for m in range(DC):
                    mm = pe.matmul(bank[:, 3, 0:WK], qTw[:, m].rearrange("p a b -> p (a b)"), kTw[:, m], start=(m == 0), stop=(m == DC - 1))
                mm.then_inc(win_s, 1)
                win_qkv(j + 1)
                pe.wait_ge(win_p, j + 1)
                pe.transpose(bank[0:WK, 4, 0:P], pw[:], ident[:]).then_inc(win_pt_ps, 1)
                pe.wait_ge(win_pt, j + 1)
                for m in range(DC):
                    mm = pe.matmul(bank[:, 5, m * P:(m + 1) * P], vw[0:WK, m * P:(m + 1) * P], pTw[0:WK, :], start=True, stop=True)
                mm.then_inc(win_c_ps, 1)
                pe.wait_ge(win_c, j + 1)
                pe.wait_ge(win_add, j)
                for m in range(DC):
                    mm = pe.matmul(bank[:, 6, 0:D], cTw[:, m], wo3_sb[:, 2 * DC + m], start=(m == 0), stop=(m == DC - 1))
                mm.then_inc(win_o, 1)
            end_phase(pe, 3)
            end_phase(pe, 4)

            with pe.Fori(0, DEPTH) as lay:
                end_phase(pe, 5 + 4 * lay)

                def transposes(g):
                    pe.wait_ge(h_staged, 2 * (g + lay) + 2)
                    for c in range(DC):
                        tr = pe.transpose(bank[:, 5, c * P:(c + 1) * P], h_in[:, c], ident[:])
                    tr.then_inc(hT_ps, 1)

                def project(f, s):
                    to, c = divmod(s, 2)
                    if s == 0:
                        pe.wait_ge(hT_hi_ready, f + lay + 1)
                        pe.wait_ge(hT_lo_ready, f + lay + 1)
                    if s == 4:
                        pe.wait_ge(v_ready, f)
                    cols = slice(to * INNER, (to + 1) * INNER)
                    pe.matmul(bank[:, to], hT_hi[:, c], wqkv_hi[:, c, cols], start=(c == 0), stop=False)
                    pe.matmul(bank[:, to], hT_hi[:, c], wqkv_lo[:, c, cols], start=False, stop=False)
                    mm = pe.matmul(bank[:, to], hT_lo[:, c], wqkv_hi[:, c, cols], start=False, stop=(c == 1))
                    if s == 3:
                        mm.then_inc(qk_raw, 1)
                    if s == 5:
                        mm.then_inc(v_raw, 1)

                def turn_qk(f):
                    for n, (which, done) in enumerate(((1, kT_ps), (0, qT_ps))):
                        pe.wait_ge(qk_ready, 2 * f + n + 1)
                        for c in range(HEADS // 2):
                            tr = pe.transpose(bank[:, which, c * P:(c + 1) * P], qk_cos[:, which, c * P:(c + 1) * P], ident[:])
                        tr.then_inc(done, 1)

                def scores(k, j):
                    if j >= 2:
                        pe.wait_ge(masked, HEADS * k + 2 * lay + 2 * j - 2)
                    for e in range(2):
                        mm = pe.matmul(bank[:, 3 + j % 2, e * 2 * P:(e + 1) * 2 * P], qT[:, j, e],
                                       kT[:, j].rearrange("p a b -> p (a b)"), start=True, stop=True)
                    mm.then_inc(s_ready, 1)

                def project_out(k, c):
                    mm = pe.matmul(bank[:, 6, 0:D], oT[:, c], wo_sb[:, c], start=(c == 0), stop=(c == INNER // P - 1))
                    if c == INNER // P - 1:
                        mm.then_inc(wo_ps, 1)

                def turn_probs(k, j):
                    if j == 1:
                        pe.wait_ge(x_attn, k)
                    if j >= 2:
                        pe.wait_ge(pt_ready, 4 * k + j - 1)
                    for h in (2 * j, 2 * j + 1):
                        pe.wait_ge((p_even, p_odd)[h % 2], HEADS // 2 * k + j + 1)
                        for c in range(2):
                            tr = pe.transpose(bank[:, 5 + j % 2, ((h % 2) * 2 + c) * P:((h % 2) * 2 + c + 1) * P], prob[:, h % 6, c], ident[:])
                    tr.then_inc(pt_ps, 1)

                def values(k, j):
                    pe.wait_ge(pt_ready, 4 * k + j + 1)
                    for c in range(2):
                        for e in range(2):
                            h = 2 * j + e
                            mm = pe.matmul(bank[e * DH:(e + 1) * DH, 7, j * P:(j + 1) * P], v_sb[:, c, h * DH:(h + 1) * DH],
                                           pT[:, j % 2, (e * 2 + c) * P:(e * 2 + c + 1) * P], start=(c == 0), stop=(c == 1))
                    mm.then_inc(pv_done, 1)

                f0 = lay * (NB + 1)
                transposes(f0 + lay)
                pe.wait_ge(wo_loaded, 16 * 8 * (lay + 1))
                for s in range(6):
                    project(f0, s)
                transposes(f0 + lay + 1)
                turn_qk(f0)
                pe.wait_ge(kT_ready, f0 + 1)
                pe.wait_ge(q_even, f0 + 1)
                pe.wait_ge(q_odd, f0 + 1)
                scores(lay * NB, 0)
                with pe.Fori(0, NB // 2) as u:
                    for i in range(2):
                        k = lay * NB + u * 2 + i
                        f = f0 + u * 2 + i + 1
                        scores(k, 1)
                        project(f, 0)
                        project(f, 1)
                        scores(k, 2)
                        project(f, 2)
                        scores(k, 3)
                        project(f, 3)
                        turn_probs(k, 0)
                        project(f, 4)
                        turn_probs(k, 1)
                        values(k, 0)
                        project(f, 5)
                        turn_probs(k, 2)
                        values(k, 1)
                        turn_probs(k, 3)
                        values(k, 2)
                        transposes(f + lay + 1)
                        values(k, 3)
                        turn_qk(f)
                        pe.wait_ge(ot_ready, k + 1)
                        project_out(k, 0)
                        project_out(k, 1)
                        pe.wait_ge(kT_ready, f + 1)
                        pe.wait_ge(q_even, f + 1)
                        pe.wait_ge(q_odd, f + 1)
                        scores(k + 1, 0)
                        project_out(k, 2)
                        project_out(k, 3)
                end_phase(pe, 6 + 4 * lay)
                end_phase(pe, 7 + 4 * lay)

                def turn_norm(n):
                    pe.wait_ge(n_norm, 8 * (n + 1))
                    for c in range(DC):
                        for i in range(GB):
                            tr = pe.transpose(bank[:, 6 + c, i * P:(i + 1) * P], hn[:, i, c * P:(c + 1) * P], ident[:])
                    tr.then_inc(nT_ps, 1)

                def up(k, j, half):
                    w = fw(j)
                    if j >= 2:
                        pe.wait_ge(g_ready, FC * k + j - 1)
                    for to, first, done in ((0, HID, g_ps), (2, 0, a_ps)):
                        if to == 2 and j >= 2:
                            pe.wait_ge(act_ready, FC * k + j - 1)
                        cols = slice(first + j * FW, first + j * FW + w)
                        for c in range(DC):
                            pe.matmul(bank[0:w, to + j % 2], w1_hi[:, c, cols], h_hi[:, half, c], start=(c == 0), stop=False)
                            pe.matmul(bank[0:w, to + j % 2], w1_lo[:, c, cols], h_hi[:, half, c], start=False, stop=False)
                            mm = pe.matmul(bank[0:w, to + j % 2], w1_hi[:, c, cols], h_lo[:, half, c], start=False, stop=(c == DC - 1))
                        mm.then_inc(done, 1)

                def down(k, j):
                    w = fw(j)
                    pe.wait_ge(act_lo_ready, FC * k + j + 1)
                    if j == 0:
                        pe.wait_ge(x_ffn, 2 * k)
                    for i in range(GB):
                        to = bank[:, 4 + i // 2, (i % 2) * D:(i % 2 + 1) * D]
                        tok = slice(i * P, (i + 1) * P)
                        pe.matmul(to, act_hi[0:w, j % 3, tok], w2_hi[0:w, j], start=(j == 0 and i % 2 == 0), stop=False, skip_group_check=True)
                        pe.matmul(to, act_hi[0:w, j % 3, tok], w2_lo[0:w, j], start=False, stop=False, skip_group_check=True)
                        mm = pe.matmul(to, act_lo[0:w, j % 3, tok], w2_hi[0:w, j], start=False, stop=(j == FC - 1), skip_group_check=True)
                    mm.then_inc(w2_used, 1)

                n0 = lay * (NG + 1)
                turn_norm(n0)
                with pe.Fori(0, NG // 2) as u:
                    for i in range(2):
                        k = lay * NG + u * 2 + i
                        n = n0 + u * 2 + i
                        pe.wait_ge(nT_lo, 2 * n + 2)
                        for j in range(FC + 2):
                            if j < FC:
                                up(k, j, i)
                            if j >= 2:
                                down(k, j - 2)
                            if j == 3:
                                turn_norm(n + 1)
                end_phase(pe, 8 + 4 * lay)

        @block.vector
        def _(dve):
            dve.wait_ge(consts_ready, 1)
            with dve.Fori(0, NG // 2) as u:
                for i in range(2):
                    g = u * 2 + i
                    dve.wait_ge(x_loaded[i], 16 * (u + 1))
                    settle(dve)
                    for b in range(GB):
                        dve.bn_stats(l_bst[:, b], x_in[:, i, b]).then_inc(l_stat_step, 1)
                    dve.wait_ge(l_stat_step, (g + 1) * GB)
                    settle(dve)
                    for b in range(GB):
                        dve.bn_aggr(l_mv[:, b], l_bst[:, b]).then_inc(l_stats, 1)
                    dve.wait_ge(l_rs, g + 1)
                    dve.wait_ge(xnT_ps, 2 * g)
                    for b in range(GB):
                        dve.tensor_scalar(xn_st[:, b], x_in[:, i, b], l_mv[:, b, 0:1], l_rstd[:, b:b + 1],
                                          ALU.subtract, ALU.mult).then_inc(l_norm, 1)
                    dve.wait_ge(l_norm, (g + 1) * GB)
                    dve.tensor_copy(x_sb[:, bass.ds(g * GB, GB), :], xn_st[:]).then_inc(l_step, 1)
            end_phase(dve, 1)

            dve.wait_ge(row_t_ps, 1)
            dve.tensor_copy(turned, bank[:, 6:8].rearrange("p a (c n) -> p (a c) n", n=64)).then_inc(row_t_ready, 1)
            dve.tensor_copy(left[:], rows[:]).then_inc(topk_step, 1)
            dve.wait_ge(gate_exp, 3)
            dve.tensor_scalar(gate[:], gate[:], 1.0, None, ALU.add).then_inc(gate_step, 1)
            dve.wait_ge(gate_step, 1)
            dve.reciprocal(gate[:], gate[:]).then_inc(gate_step, 1)
            dve.wait_ge(gate_step, 2)
            dve.tensor_reduce(gsum[:], gate[:], AX_X, ALU.add).then_inc(gate_step, 1)
            dve.wait_ge(gate_step, 3)
            dve.tensor_scalar(gsum[:], gsum[:], 1e-6, None, ALU.add).then_inc(gate_step, 1)
            dve.wait_ge(gate_step, 4)
            dve.reciprocal(gsum[:], gsum[:]).then_inc(gate_step, 1)
            dve.wait_ge(gate_step, 5)
            dve.tensor_tensor(gate[:], gate[:], gsum[:, :, :, None].broadcast_to([P, BPB, B, 3]), ALU.mult).then_inc(gates_ready, 1)
            dve.wait_ge(gates_ready, 1)
            dve.wait_ge(w_loaded, 16 * NLOAD)

            def topk_round(r):
                dve.wait_ge(topk_step, 2 * r + 1)
                dve.max(top8[:], left[:]).then_inc(topk_step, 1)
                dve.wait_ge(topk_step, 2 * r + 2)
                dve.match_replace(left[:], top8[:], left[:], MARK).then_inc(topk_step, 1)

            rounds = 0
            for job, (T, b, at, n0) in enumerate(JOBS):
                if T == NCOMP:
                    for _ in range(5):
                        topk_round(rounds)
                        rounds += 1
                elif b == 0:
                    while rounds < ROUNDS:
                        topk_round(rounds)
                        rounds += 1
                    dve.wait_ge(topk_step, 2 * ROUNDS + 1)
                    dve.tensor_scalar(left[:], left[:], MARK, None, ALU.is_equal).then_inc(topk_step, 1)
                    dve.wait_ge(topk_step, 2 * ROUNDS + 2)
                    dve.tensor_tensor_scan(place_row[:], left[:], left[:], 0.0, ALU.add, ALU.max).then_inc(topk_step, 1)
                    dve.wait_ge(topk_step, 2 * ROUNDS + 3)
                    dve.tensor_tensor(place_row[:], place_row[:], left[:], ALU.mult).then_inc(topk_step, 1)
                    dve.wait_ge(pos_ps, 1)
                    dve.tensor_copy(turned, bank[:, 6:8].rearrange("p a (c n) -> p (a c) n", n=64)).then_inc(pos_ready, 1)
                    dve.wait_ge(pos_ready, 1)
                if T != NCOMP:
                    for c in range(BPB):
                        n = b * BPB + c
                        if n >= 2:
                            dve.wait_ge(sel_used, n - 1)
                        dve.tensor_scalar(sel_m[:, n % 2], iota1[:], turned[:, c, 32 * b:32 * b + 1], None, ALU.is_equal).then_inc(sel_made, 1)
                dve.wait_ge(com_v_ps, job + 1)
                dve.tensor_tensor(vc[:, 0:T // P], bank[:, 0:2].rearrange("p a (k d) -> p (a k) d", d=D)[:, 0:T // P],
                                  bv_bc[:, None, :].broadcast_to([P, T // P, D]), ALU.add).then_inc(com_v, 1)
                for qb in range(T // P):
                    n = n0 + qb
                    if T == NCOMP and rounds < ROUNDS - 1:
                        topk_round(rounds)
                        rounds += 1
                    dve.wait_ge(com_s, n + 1)
                    dve.tensor_reduce(c_max[:, 0:1], bank[:, 6, 0:T], AX_X, ALU.max).then_inc(com_m, 1)
                    dve.wait_ge(com_m, n + 1)
                    dve.tensor_scalar(c_max[:, 1:2], c_max[:, 0:1], -SCALE, None, ALU.mult).then_inc(com_nm, 1)
                    dve.wait_ge(com_e, n + 1)
                    dve.reciprocal(c_max[:, 3:4], c_max[:, 2:3]).then_inc(com_f, 1)
                    dve.wait_ge(com_f, 2 * n + 1)
                    which = 0 if T == NCOMP else 1
                    dve.tensor_tensor(c_max[:, 3:4], c_max[:, 3:4], gate[:, qb, b, which:which + 1], ALU.mult).then_inc(com_f, 1)
                    dve.wait_ge(com_f, 2 * n + 2)
                    dve.tensor_scalar(pc[:, 0:T], pc[:, 0:T], c_max[:, 3:4], None, ALU.mult).then_inc(com_p, 1)
            for n in range(B * (NCOMP // P)):
                b, qb = divmod(n, NCOMP // P)
                dve.wait_ge(com_o, n + 1)
                dve.tensor_tensor(x_sb[:, b * BPB + qb], bank[:, 6, 0:D], x_sb[:, b * BPB + qb], ALU.add).then_inc(com_add, 1)
            end_phase(dve, 2)

            def win_values(j):
                dve.wait_ge(win_v_ps, j + 1)
                dve.wait_ge(win_c_ps, j)
                dve.tensor_tensor(vw[0:WK, :], bank[0:WK, 2, 0:D], bv_bc[0:WK, :], ALU.add).then_inc(win_v, 1)

            win_values(0)
            with dve.Fori(0, NB) as j:
                dve.wait_ge(win_s, j + 1)
                dve.wait_ge(win_pt_ps, j)
                settle(dve)
                dve.tensor_tensor_reduce(pw[:], bank[:, 3, 0:WK], mask_win[:], 1.0, MARK, ALU.add, ALU.max, w_max[:, 0:1]).then_inc(win_m, 1)
                dve.wait_ge(win_m, j + 1)
                dve.tensor_scalar(w_max[:, 1:2], w_max[:, 0:1], -SCALE, None, ALU.mult).then_inc(win_nm, 1)
                dve.wait_ge(win_e, j + 1)
                dve.reciprocal(w_max[:, 3:4], w_max[:, 2:3]).then_inc(win_f, 1)
                dve.wait_ge(win_f, 2 * j + 1)
                dve.tensor_tensor(w_max[:, 3:4], w_max[:, 3:4], gate[:, j % BPB, j // BPB, 2:3], ALU.mult).then_inc(win_f, 1)
                dve.wait_ge(win_f, 2 * j + 2)
                dve.tensor_scalar(pw[:], pw[:], w_max[:, 3:4], None, ALU.mult).then_inc(win_p, 1)
                win_values(j + 1)
                dve.wait_ge(win_o, j + 1)
                dve.wait_ge(bo_added, j + 1)
                dve.tensor_tensor(x_sb[:, j, :], bank[:, 6, 0:D], x_sb[:, j, :], ALU.add).then_inc(win_add, 1)
            end_phase(dve, 3)

            with dve.Fori(0, NG // 2) as u:
                for i in range(2):
                    g = u * 2 + i
                    xg = lambda b: x_sb[:, g * GB + b, :]
                    for b in range(GB):
                        dve.bn_stats(l_bst[:, b], xg(b)).then_inc(l_stat_step, 1)
                    dve.wait_ge(l_stat_step, NB + 2 * g * GB + GB)
                    settle(dve)
                    for b in range(GB):
                        dve.bn_aggr(l_mv[:, b], l_bst[:, b]).then_inc(l_norm2, 1)
                    dve.wait_ge(l_norm2, 3 * g * GB + GB)
                    dve.tensor_scalar(l_t[:, 0], l_mv[:, :, 1], 0.25, None, ALU.mult).then_inc(l_step, 1)
                    dve.wait_ge(l_rs, NG + 3 * g + 1)
                    dve.tensor_tensor(l_t[:, 4], l_t[:, 0], l_t[:, 1], ALU.mult).then_inc(l_step, 1)
                    dve.wait_ge(l_step, NG + 4 * g + 2)
                    dve.tensor_tensor(l_t[:, 2], l_t[:, 4], l_t[:, 1], ALU.mult).then_inc(l_step, 1)
                    dve.wait_ge(l_rs, NG + 3 * g + 2)
                    dve.scalar_tensor_tensor(out=l_t[:, 5], in0=l_t[:, 1], scalar=0.5, in1=l_t[:, 3], op0=ALU.mult, op1=ALU.mult).then_inc(l_step, 1)
                    dve.wait_ge(l_step, NG + 4 * g + 4)
                    settle(dve)
                    for b in range(GB):
                        dve.tensor_scalar(xn_st[:, b], xg(b), l_mv[:, b, 0:1], l_t[:, 5, b:b + 1], ALU.subtract, ALU.mult).then_inc(l_norm2, 1)
                    dve.wait_ge(l_norm2, 3 * g * GB + 2 * GB)
                    dve.wait_ge(x_loaded[i], 16 * (NG // 2 + u + 1))
                    dve.tensor_tensor(x_in[:, i], x_in[:, i], xn_st[:], ALU.add).then_inc(l_x1, 1)
                    dve.wait_ge(l_x1, g + 1)
                    settle(dve)
                    for b in range(GB):
                        dve.bn_stats(l_bst[:, b], x_in[:, i, b]).then_inc(l_stat_step, 1)
                    dve.wait_ge(l_stat_step, NB + 2 * g * GB + 2 * GB)
                    settle(dve)
                    for b in range(GB):
                        dve.bn_aggr(l_mv[:, b], l_bst[:, b]).then_inc(l_norm2, 1)
                    dve.wait_ge(l_rs, NG + 3 * g + 3)
                    for b in range(GB):
                        dve.tensor_scalar(xg(b), x_in[:, i, b], l_mv[:, b, 0:1], l_rstd[:, b:b + 1], ALU.subtract, ALU.mult).then_inc(l_xf, 1)
            end_phase(dve, 4)

            with dve.Fori(0, DEPTH) as lay:
                for c in range(DC):
                    dve.wait_ge(split_hi, 6 * lay + c + 1)
                    dve.tensor_tensor(wqkv_lo[:, c], raw[:, c], wqkv_hi[:, c], ALU.subtract).then_inc(split_lo, 1)
                dve.memset(qT[:], 0.0).then_inc(kv_zero, 1)
                dve.memset(kT[:, :, 1], 0.0).then_inc(kv_zero, 1)
                dve.memset(v_sb[:, 1], 0.0).then_inc(kv_zero, 1)
                end_phase(dve, 5 + 4 * lay)

                def lo(g):
                    dve.wait_ge(hT_hi_ready, g + 1)
                    dve.tensor_tensor(hT_lo[:], bank[:, 5, 0:2 * P].rearrange("p (c t) -> p c t", c=DC), hT_hi[:], ALU.subtract).then_inc(hT_lo_ready, 1)

                def cosines(f, t):
                    dve.wait_ge(squares, f + 1)
                    dve.tensor_tensor(qk_cos[:].rearrange("p a (h d) -> p a h d", d=DH),
                                      bank[:, 0:2].rearrange("p a (h d) -> p a h d", d=DH),
                                      rope[:, t % BPB, 0][:, :, None, :].broadcast_to([P, 2, HEADS, DH]), ALU.mult).then_inc(rotated, 1)

                def sines(t, which):
                    dve.tensor_tensor(qk_sin[:, which].rearrange("p (h a d) -> p h a d", a=2, d=DH // 2),
                                      bank[:, which].rearrange("p (h a d) -> p h a d", a=2, d=DH // 2)[:, :, ::-1, :],
                                      rope[:, t % BPB, 1, which].rearrange("p (a d) -> p a d", a=2)[:, None, :, :].broadcast_to([P, HEADS, 2, DH // 2]),
                                      ALU.mult).then_inc(rotated, 1)

                def sums(f):
                    dve.wait_ge(squares, f + 1)
                    dve.tensor_reduce(sumsq[:], qk_sq[:].rearrange("p a (h d) -> p (a h) d", d=DH), AX_X, ALU.add).then_inc(ss_ready, 1)

                def floor_sums(f):
                    dve.wait_ge(ss_ready, f + 1)
                    settle(dve)
                    dve.tensor_scalar(sumsq[:], sumsq[:], 1e-24, None, ALU.max).then_inc(ss_floor, 1)

                def add_k(f):
                    dve.wait_ge(rotated, 3 * f + 2)
                    dve.tensor_tensor(qk_cos[:, 1], qk_cos[:, 1], qk_sin[:, 1], ALU.add).then_inc(zk_ready, 1)

                def normalise(f, which):
                    dve.wait_ge(r_ready, f + 1)
                    dve.wait_ge((zq_ready, zk_ready)[which], f + 1)
                    z = qk_cos[:, which].rearrange("p (h d) -> p h d", d=DH)
                    dve.tensor_tensor(z, z, rnorm[:, which * HEADS:(which + 1) * HEADS, None].broadcast_to([P, HEADS, DH]), ALU.mult).then_inc(qk_ready, 1)

                def k_out(f, half):
                    dve.wait_ge(kT_ps, f + 1)
                    dve.tensor_copy(kT[:, :, half], bank[:, 1].rearrange("p (c t) -> p c t", t=P)).then_inc(kT_ready, 1)
                    dve.wait_ge(qT_ps, f + 1)
                    dve.tensor_copy(qT[0:DH, :, 0], bank[0:DH, 0].rearrange("p (c t) -> p c t", t=P)).then_inc(q_even, 1)

                f0 = lay * (NB + 1)

                def hide(i, k, h):
                    mask = (mask_even, mask_odd)[i]
                    dve.wait_ge(s_ready, 4 * k + lay + h // 2 + 1)
                    if h >= 6:
                        dve.wait_ge(pt_ps, 4 * k + 1)
                    settle(dve)
                    dve.tensor_tensor_reduce(prob[:, h % 6].rearrange("p a b -> p (a b)"), bank[:, 3 + (h // 2) % 2, (h % 2) * 2 * P:(h % 2 + 1) * 2 * P],
                                             mask[:].rearrange("p a b -> p (a b)"), 1.0, 3e38, ALU.add, ALU.min, neg_max[:, h:h + 1]).then_inc(masked, 1)

                lo(f0 + lay)
                cosines(f0, 0)
                sums(f0)
                floor_sums(f0)
                sines(0, 1)
                sines(0, 0)
                add_k(f0)
                normalise(f0, 1)
                lo(f0 + lay + 1)
                normalise(f0, 0)
                k_out(f0, 0)
                dve.wait_ge(mask_set, lay * (NB // 2 + 1) + 1)
                hide(0, lay * NB, 0)
                hide(0, lay * NB, 1)
                with dve.Fori(0, NB // 2) as u:
                    for i in range(2):
                        t = u * 2 + i
                        k = lay * NB + t
                        f = f0 + t + 1
                        def weigh(h):
                            for e in range(2):
                                dve.wait_ge(exped, HEADS * k + h + e + 1)
                                dve.reciprocal(pinv[:, h + e:h + e + 1], psums[:, h + e:h + e + 1]).then_inc(inverted, 1)
                            dve.wait_ge(inverted, HEADS * k + h + 1)
                            dve.tensor_scalar(prob[:, h % 6], prob[:, h % 6], pinv[:, h:h + 1], None, ALU.mult).then_inc(p_even, 1)

                        hide(i, k, 2)
                        hide(i, k, 3)
                        weigh(0)
                        hide(i, k, 4)
                        hide(i, k, 5)
                        weigh(2)
                        hide(i, k, 6)
                        hide(i, k, 7)
                        sums(f)
                        weigh(4)
                        floor_sums(f)
                        cosines(f, t + 1)
                        weigh(6)
                        sines(t + 1, 1)
                        sines(t + 1, 0)
                        add_k(f)
                        normalise(f, 1)
                        lo(f + lay + 1)
                        normalise(f, 0)
                        k_out(f, 1 - i)
                        if i == 1:
                            dve.wait_ge(mask_set, lay * (NB // 2 + 1) + u + 2)
                        hide(1 - i, k + 1, 0)
                        hide(1 - i, k + 1, 1)
                        dve.wait_ge(wo_ps, k + 1)
                        dve.tensor_tensor(x_sb[:, t, :], bank[:, 6, 0:D], x_sb[:, t, :], ALU.add).then_inc(x_attn, 1)
                end_phase(dve, 6 + 4 * lay)

                for c in range(DC):
                    dve.wait_ge(split_hi, 6 * lay + 2 + c + 1)
                    dve.tensor_tensor(w1_lo[:, c], raw[:, c, 0:2 * HID], w1_hi[:, c], ALU.subtract).then_inc(split_lo, 1)
                raw_w2 = raw[:, 2, :].rearrange("p (c n) -> p c n", n=D)
                dve.wait_ge(split_hi, 6 * lay + 6)
                dve.tensor_tensor(w2_lo[0:FW, 0:FC - 1], raw_w2[0:FW, 0:FC - 1], w2_hi[0:FW, 0:FC - 1], ALU.subtract).then_inc(split_lo, 1)
                dve.tensor_tensor(w2_lo[0:fw(FC - 1), FC - 1], raw_w2[0:fw(FC - 1), FC - 1], w2_hi[0:fw(FC - 1), FC - 1], ALU.subtract).then_inc(split_lo, 1)
                end_phase(dve, 7 + 4 * lay)

                def norm_stats(n, g):
                    for b in range(GB):
                        t = g * GB + b
                        dve.bn_stats(bst[:, b, 0], x_sb[:, t, 0:P]).then_inc(n_stats, 1)
                        dve.bn_stats(bst[:, b, 1], hs_ffn[:, t + t // BPB, :]).then_inc(n_stats, 1)
                    dve.wait_ge(n_stats, 2 * GB * (n + 1))
                    settle(dve)
                    for b in range(GB):
                        dve.bn_aggr(mv[:, b], bst[:, b].rearrange("p a s -> p (a s)")).then_inc(n_aggr, 1)

                def norm_apply(n, g):
                    dve.wait_ge(n_rs, n + 1)
                    dve.wait_ge(nT_ps, n)
                    settle(dve)
                    for b in range(GB):
                        t = g * GB + b
                        for c, src in enumerate((x_sb[:, t, 0:P], hs_ffn[:, t + t // BPB, :])):
                            dve.tensor_scalar(hn[:, b, c * P:(c + 1) * P], src, mv[:, b, 0:1], rstd[:, b:b + 1],
                                              ALU.subtract, ALU.mult).then_inc(n_norm, 1)

                def norm_full(n):
                    dve.wait_ge(nT_lo, 2 * n)
                    for c in range(DC):
                        dve.wait_ge(nT_hi, 2 * n + c + 1)
                        dve.tensor_scalar(h_full[:, c], bank[:, 6 + c], ln_gb[:, 0, c:c + 1], ln_gb[:, 1, c:c + 1], ALU.mult, ALU.add).then_inc(nT_full, 1)

                n0 = lay * (NG + 1)
                dve.wait_ge(wo_loaded, 16 * 8 * (lay + 1))
                norm_stats(n0, 0)
                norm_apply(n0, 0)
                norm_full(n0)
                with dve.Fori(0, NG // 2) as u:
                    for i in range(2):
                        g = u * 2 + i
                        k = lay * NG + g
                        n = n0 + g + 1
                        for j in range(FC):
                            w = fw(j)
                            dve.wait_ge(a_ps, FC * k + j + 1)
                            dve.wait_ge(g_ready, FC * k + j + 1)
                            if j >= 2:
                                dve.wait_ge(act_lo_ready, FC * k + j - 1)
                            dve.scalar_tensor_tensor(out=act_full[0:w, j % 2], in0=bank[0:w, 2 + j % 2], scalar=b1_sb[0:w, 0, j:j + 1],
                                                     in1=gelu_sb[0:w, j % 2], op0=ALU.add, op1=ALU.mult).then_inc(act_ready, 1)
                            if j >= 3:
                                dve.wait_ge(w2_used, FC * k + j - 2)
                            dve.wait_ge(act_ready, FC * k + j + 1)
                            dve.tensor_copy(act_hi[0:w, j % 3], act_full[0:w, j % 2]).then_inc(act_hi_ready, 1)
                            if j == 0:
                                norm_stats(n, (g + 1) % NG)
                            if j == 2:
                                norm_apply(n, (g + 1) % NG)
                            if j == 4:
                                norm_full(n)
                        dve.wait_ge(w2_used, FC * (k + 1))
                        dve.wait_ge(b2_added, k + 1)
                        for h in range(2):
                            xs = x_sb[:, bass.ds(g * GB + 2 * h, 2), :]
                            dve.tensor_tensor(xs, bank[:, 4 + h].rearrange("p (b d) -> p b d", d=D), xs, ALU.add).then_inc(x_ffn, 1)
                end_phase(dve, 8 + 4 * lay)

            with dve.Fori(0, NG // 2) as u:
                for i in range(2):
                    g = u * 2 + i
                    for b in range(GB):
                        dve.bn_stats(f_bst[:, b], x_sb[:, g * GB + b, :]).then_inc(f_step, 1)
                    dve.wait_ge(f_step, (g + 1) * GB)
                    settle(dve)
                    for b in range(GB):
                        dve.bn_aggr(f_mv[:, i, b], f_bst[:, b]).then_inc(f_stats, 1)
                    dve.wait_ge(f_rs, g + 1)
                    dve.wait_ge(out_stored[i], 16 * u)
                    settle(dve)
                    for b in range(GB):
                        dve.tensor_scalar(f_y[:, i, b], x_sb[:, g * GB + b, :], f_mv[:, i, b, 0:1], f_rstd[:, i, b:b + 1], ALU.subtract, ALU.mult).then_inc(f_norm, 1)
                    dve.wait_ge(f_norm, (g + 1) * GB)
                    dve.wait_ge(f_x1_loaded[i], 16 * (u + 1))
                    dve.tensor_tensor(f_y[:, i], f_y[:, i], f_x1[:, i], ALU.add).then_inc(f_sum, 1)


_INS = ["L0_attn_hidden_states", "L0_attn_Wq", "L0_attn_bq", "L0_attn_Wk", "L0_attn_bk", "L0_attn_Wv", "L0_attn_bv", "L0_attn_Wo",
        "L0_attn_bo", "L0_attn_Wg", "L0_attn_bg", "L0_attn_Wc", "L0_attn_bc", "L0_attn_Ws", "L0_attn_bs", "L0_ffn_wqkv",
        "L0_ffn_q_scale", "L0_ffn_k_scale", "L0_ffn_wo", "L0_ffn_ln_g", "L0_ffn_ln_b", "L0_ffn_w1", "L0_ffn_b1", "L0_ffn_w2", "L0_ffn_b2"]


def rope_constants():
    half = np.arange(0, DH, 2, dtype=np.float32)
    inv_freq = (1.0 / 10000.0 ** (half / DH)).astype(np.float32)
    t = np.arange(N, dtype=np.float32)
    freqs = (t[:, None] * inv_freq[None, :]).astype(np.float32).astype(np.float64)
    base = (half + 0.4 * DH).astype(np.float64) / (1.4 * DH)
    scale = base[None, :] ** (((t - N // 2) / 64.0).astype(np.float64))[:, None]
    tab = np.stack([np.stack([f(freqs) * scale, f(freqs) / scale], 1) for f in (np.cos, np.sin)])
    tab = tab.reshape(2, BPB, P, 2, DH // 2).transpose(2, 0, 1, 3, 4)
    return np.ascontiguousarray(tab.reshape(P, 2, BPB * 64)).astype(np.float32)


def kernel(**inputs):
    import concourse.bacc as _bacc
    from concourse.bass_utils import run_bass_kernel_spmd as _run

    nc = _bacc.Bacc("TRN2", target_bir_lowering=False, num_devices=1)
    arrays, args = {}, []
    for name in _INS:
        a = np.ascontiguousarray(inputs[name])
        arrays[f"in_{name}"] = a
        args.append(nc.dram_tensor(f"in_{name}", a.shape, mybir.dt.from_np(a.dtype), kind="ExternalInput").ap())
    arrays["rope_base"] = rope_constants()
    args.append(nc.dram_tensor("rope_base", arrays["rope_base"].shape, F32, kind="ExternalInput").ap())
    args.append(nc.dram_tensor("out", (B, N, D), F32, kind="ExternalOutput").ap())
    build(nc, *args)
    r = _run(nc, [arrays], core_ids=[0])
    return r.results[0]["out"]
```

```python
from contextlib import ExitStack

import numpy as np

import concourse.bass as bass
from concourse import mybir

ALU = mybir.AluOpType
ACT = mybir.ActivationFunctionType
F32 = mybir.dt.float32
F32R = mybir.dt.float32r
AX_X = mybir.AxisListType.X

P = 128
B, N, D = 2, 2048, 256
DC = D // P
NB = B * N // P
BPB = N // P
GB = 4
NG = NB // GB
GPB = NG // B
GT = GB * P

RATIO, SEL, WIN = 4, 128, 64
NCOMP = N // RATIO
SCALE = 0.25
WK = WIN + WIN // 2
ROUNDS = SEL // 8

DEPTH, HEADS, DH = 2, 8, 64
INNER = HEADS * DH
QK_SCALE = 8.0
HID = 682
FC = 6
FW = 114
BIG = 1e30
MARK = -3.4e38


def fw(j):
    return min(FW, HID - j * FW)


SHARE = 3 * INNER // (NG // 2)
SPLITS = 4 + NG // 2


def hs_slot(t):
    return t + t // BPB


def build(nc, x0, Wq, bq, Wk, bk, Wv, bv, Wo, bo, Wg, bg, Wc, bc, Ws, bs,
          wqkv, q_scale, k_scale, wo, ln_g, ln_b, w1, b1, w2, b2, rope_base, out):
    with ExitStack() as ctx:
        base = [(nc.sbuf_base + 63) // 64 * 64]

        def place(name, shape, dt=F32):
            size = 4 * int(np.prod(shape[1:]))
            at = base[0]
            base[0] += (size + 31) // 32 * 32
            assert base[0] <= nc.sbuf_top, (name, base[0])
            return nc.alloc_sbuf_tensor_at(name, shape, dt, offset=at)

        def sem(name):
            return ctx.enter_context(nc.semaphore(name))

        x_sb = place("x_sb", [P, NB, D])
        hs_attn = place("hs_attn", [P, NB + B, P])
        hs_ffn = place("hs_ffn", [P, NB + B, P])
        ident = place("ident", [P, P])
        mask_tab = place("mask_tab", [P, 2, P])
        mask_odd = place("mask_odd", [P, 2, P])
        mask_even = place("mask_even", [P, 2, P])
        neg_half = place("neg_half", [P, 16])
        warm = place("warm", [P, 1])
        raw = place("raw", [P, 3, 1536])
        qk_sc = place("qk_sc", [P, 2, DH])
        zero = place("zero", [P, 1])
        stage0_base = base[0]

        rope_at = base[0]
        rope = place("rope", [P, BPB, 2, 2, DH])
        wqkv_hi = place("wqkv_hi", [P, DC, 3 * INNER], F32R)
        wqkv_lo = place("wqkv_lo", [P, DC, 3 * INNER], F32R)
        wo_sb = place("wo_sb", [P, INNER // P, D])
        w1_hi = place("w1_hi", [P, DC, 2 * HID], F32R)
        w1_lo = place("w1_lo", [P, DC, 2 * HID], F32R)
        w2_hi = place("w2_hi", [P, FC, D], F32R)
        w2_lo = place("w2_lo", [P, FC, D], F32R)
        sc_x = place("sc_x", [P, 2, 2, DH])
        ln_gb = place("ln_gb", [P, 2, DC])
        b1_sb = place("b1_sb", [P, 2, FC])
        b2_sb = place("b2_sb", [P, D])
        work_base = base[0]
        h_in = place("h_in", [P, DC, P])
        hT_hi = place("hT_hi", [P, DC, P], F32R)
        hT_lo = place("hT_lo", [P, DC, P], F32R)
        qk_cos = place("qk_cos", [P, 2, INNER])
        qk_sin = place("qk_sin", [P, 2, INNER])
        qk_sq = qk_sin
        sumsq = place("sumsq", [P, 2 * HEADS])
        rnorm = place("rnorm", [P, 2 * HEADS])
        qT = place("qT", [P, HEADS // 2, 2, P])
        kT = place("kT", [P, HEADS // 2, 2, P])
        v_sb = place("v_sb", [P, 2, INNER])
        prob = place("prob", [P, HEADS, 2, P])
        neg_max = place("neg_max", [P, HEADS])
        psums = place("psums", [P, HEADS])
        pinv = place("pinv", [P, HEADS])
        pT = place("pT", [P, 2, 4 * P])
        oT = place("oT", [P, INNER // P, P])
        base[0] = rope_at
        hn = place("hn", [P, GB, D])
        h_full = place("h_full", [P, DC, GT])
        gelu_sb = place("gelu_sb", [P, 2, GT])
        act_full = place("act_full", [P, 2, GT])
        base[0] = work_base
        h_hi = place("h_hi", [P, 2, DC, GT], F32R)
        h_lo = place("h_lo", [P, 2, DC, GT], F32R)
        act_hi = place("act_hi", [P, 3, GT], F32R)
        act_lo = place("act_lo", [P, 3, GT], F32R)
        bst = place("bst", [P, GB, 2, 6])
        mv = place("mv", [P, GB, 2])
        rstd = place("rstd", [P, GB])
        base[0] = work_base
        f_x1 = place("f_x1", [P, 2, GB, D])
        f_y = place("f_y", [P, 2, GB, D])
        f_bst = place("f_bst", [P, 2, GB, 6])
        f_mv = place("f_mv", [P, 2, GB, 2])
        f_rstd = place("f_rstd", [P, 2, GB])

        base[0] = stage0_base
        xnT = place("xnT", [P, DC, B * N])
        wq_sb = place("wq_sb", [P, DC, D])
        wk_sb = place("wk_sb", [P, DC, D])
        wv_sb = place("wv_sb", [P, DC, D])
        wc_sb = place("wc_sb", [P, RATIO * DC, D])
        wo3_sb = place("wo3_sb", [P, 3 * DC, D])
        wsg_sb = place("wsg_sb", [P, DC, 36])
        bsg_sb = place("bsg_sb", [P, 1])
        bqkc_sb = place("bqkc_sb", [P, 3, DC])
        bv_bc = place("bv_bc", [P, D])
        bo_bc = place("bo_bc", [P, D])
        rows = place("rows", [64, N])
        left = place("left", [64, N])
        place_row = place("place_row", [64, N])
        top8 = place("top8", [64, 8])
        iota1 = place("iota1", [P, P])
        turned = raw[:, 2, 0:BPB * 64].rearrange("p (c n) -> p c n", n=64)
        gate = place("gate", [P, BPB, B, 3])
        gsum = place("gsum", [P, BPB, B])
        mask_win = place("mask_win", [P, WK])
        after_const = base[0]
        base[0] = max(after_const, work_base)
        after_const = base[0]
        x_in = place("x_in", [P, 2, GB, D])
        xn_st = place("xn_st", [P, GB, D])
        l_bst = place("l_bst", [P, 2, GB, 6])
        l_mv = place("l_mv", [P, 2, GB, 2])
        l_rstd = place("l_rstd", [P, 2, GB])
        x0_in = x_in[:].rearrange("p a b d -> p (a b) d")
        m_bst = place("m_bst", [P, 6])
        m_mv = place("m_mv", [P, 2])
        m_t = place("m_t", [P, 6])
        m_scale = place("m_scale", [P, 1])
        f_bst1 = place("f_bst1", [P, 6])
        f_mv1 = place("f_mv1", [P, 2])
        f_r = place("f_r", [P, 1])
        xw = place("xw", [P, DC, WK])
        qTw = place("qTw", [P, DC, 2, WIN])
        kTw = place("kTw", [P, DC, WK])
        vw = place("vw", [P, D])
        pw = place("pw", [P, WK])
        w_max = place("w_max", [P, 4])
        pTw = place("pTw", [P, P])
        cTw = place("cTw", [P, DC, P])
        base[0] = after_const
        tokT = place("tokT", [P, DC, NCOMP])
        qTc = place("qTc", [P, DC, NCOMP])
        kTc = place("kTc", [P, DC, NCOMP])
        vc = place("vc", [P, NCOMP // P, D])
        pc = place("pc", [P, NCOMP])
        pTc = place("pTc", [P, NCOMP // P, NCOMP])
        c_max = place("c_max", [P, 4])
        sel_m = place("sel_m", [P, 2, P])
        cT = place("cT", [P, DC, B * NCOMP + B * P])

        bank = ctx.enter_context(nc.psum_tensor("bank", [P, 8, 512], F32))
        x1_dram = nc.dram_tensor("x1_scratch", [NB, P, D], F32, kind="Internal").ap()

        consts_ready = sem("consts_ready")
        phase_done = sem("phase_done")
        waited = sem("waited")

        def settle(eng):
            eng.sem_inc(waited, 1)

        def arrive(eng):
            eng.drain().then_inc(phase_done, 1)

        def await_phase(eng, n):
            eng.wait_ge(phase_done, 5 * n)
            settle(eng)

        def end_phase(eng, n):
            arrive(eng)
            await_phase(eng, n)

        w_loaded = sem("w_loaded")
        w_small = sem("w_small")
        x_loaded = [sem("x_loaded0"), sem("x_loaded1")]
        l_stats = sem("l_stats")
        l_stat_step = sem("l_stat_step")
        l_eps = sem("l_eps")
        l_rs = sem("l_rs")
        l_norm = sem("l_norm")
        l_copied = sem("l_copied")
        x0_loaded = sem("x0_loaded")
        m_stats = sem("m_stats")
        m_aggr = sem("m_aggr")
        m_step = sem("m_step")
        m_scaled = sem("m_scaled")
        m_norm = sem("m_norm")
        x1_made = sem("x1_made")
        x1_stats = sem("x1_stats")
        x1_aggr = sem("x1_aggr")
        x1_step = sem("x1_step")
        x1_root = sem("x1_root")
        x_made = sem("x_made")
        xnT_ps = sem("xnT_ps")
        xnT_ready = sem("xnT_ready")
        rows_zero = sem("rows_zero")
        rows_ps = sem("rows_ps")
        rows_ready = sem("rows_ready")
        x1_stored = sem("x1_stored")
        hs_moved = sem("hs_moved")
        row_t_ps = sem("row_t_ps")
        row_t_ready = sem("row_t_ready")
        gate_step = sem("gate_step")
        gate_exp = sem("gate_exp")
        win_x = sem("win_x")
        win_q_ps = sem("win_q_ps")
        win_k_ps = sem("win_k_ps")
        win_v_ps = sem("win_v_ps")
        win_q = sem("win_q")
        win_k = sem("win_k")
        win_v = sem("win_v")
        win_s = sem("win_s")
        win_m = sem("win_m")
        win_e = sem("win_e")
        win_f = sem("win_f")
        win_p = sem("win_p")
        win_pt_ps = sem("win_pt_ps")
        win_pt = sem("win_pt")
        win_c_ps = sem("win_c_ps")
        win_c = sem("win_c")
        win_o = sem("win_o")
        win_add = sem("win_add")
        topk_step = sem("topk_step")
        pos_ps = sem("pos_ps")
        pos_ready = sem("pos_ready")
        tok_ps = sem("tok_ps")
        tok_ready = sem("tok_ready")
        com_qk_ps = sem("com_qk_ps")
        com_qk = sem("com_qk")
        com_v_ps = sem("com_v_ps")
        com_v = sem("com_v")
        com_s = sem("com_s")
        com_m = sem("com_m")
        com_nm = sem("com_nm")
        com_e = sem("com_e")
        com_f = sem("com_f")
        com_p = sem("com_p")
        com_pt_ps = sem("com_pt_ps")
        com_pt = sem("com_pt")
        com_c_ps = sem("com_c_ps")
        com_c = sem("com_c")
        sel_made = sem("sel_made")
        sel_used = sem("sel_used")
        com_o = sem("com_o")
        com_add = sem("com_add")
        bo_added = sem("bo_added")
        raw_attn = sem("raw_attn")
        raw_ffn = sem("raw_ffn")
        split_hi = sem("split_hi")
        wo_loaded = sem("wo_loaded")
        sc_made = sem("sc_made")
        kv_zero = sem("kv_zero")
        h_staged = sem("h_staged")
        mask_set = sem("mask_set")
        hT_ps = sem("hT_ps")
        hT_hi_ready = sem("hT_hi_ready")
        hT_lo_ready = sem("hT_lo_ready")
        qk_raw = [sem("q_raw"), sem("k_raw")]
        v_raw = sem("v_raw")
        squares = [sem("squares_q"), sem("squares_k")]
        rotated = [sem("rotated_q"), sem("rotated_k")]
        ss_ready = [sem("ss_ready_q"), sem("ss_ready_k")]
        ss_floor = [sem("ss_floor_q"), sem("ss_floor_k")]
        r_ready = [sem("r_ready_q"), sem("r_ready_k")]
        z_ready = [sem("z_ready_q"), sem("z_ready_k")]
        qk_ready = [sem("q_ready"), sem("k_ready")]
        qkT_ps = [sem("qT_ps"), sem("kT_ps")]
        kT_ready = sem("kT_ready")
        q_even = sem("q_even")
        q_odd = sem("q_odd")
        v_ready = sem("v_ready")
        s_ready = sem("s_ready")
        masked = sem("masked")
        exped = sem("exped")
        inverted = sem("inverted")
        p_even = sem("p_even")
        p_odd = sem("p_odd")
        pt_ps = sem("pt_ps")
        pt_ready = sem("pt_ready")
        pv_done = sem("pv_done")
        ot_ready = sem("ot_ready")
        wo_ps = sem("wo_ps")
        x_attn = sem("x_attn")
        hs_ffn_moved = sem("hs_ffn_moved")
        n_stats = sem("n_stats")
        n_aggr = sem("n_aggr")
        n_eps = sem("n_eps")
        n_rs = sem("n_rs")
        n_norm = sem("n_norm")
        nT_ps = sem("nT_ps")
        nT_hi = sem("nT_hi")
        nT_full = sem("nT_full")
        nT_lo = sem("nT_lo")
        g_ps = sem("g_ps")
        a_ps = sem("a_ps")
        g_ready = sem("g_ready")
        act_ready = sem("act_ready")
        act_hi_ready = sem("act_hi_ready")
        act_lo_ready = sem("act_lo_ready")
        w2_used = sem("w2_used")
        b2_added = sem("b2_added")
        x_ffn = sem("x_ffn")
        hs_attn_moved = sem("hs_attn_moved")
        small_loaded = sem("small_loaded")
        f_x1_loaded = [sem("f_x1_loaded0"), sem("f_x1_loaded1")]
        f_stats = sem("f_stats")
        f_step = sem("f_step")
        f_eps = sem("f_eps")
        f_rs = sem("f_rs")
        f_norm = sem("f_norm")
        f_sum = sem("f_sum")
        out_stored = [sem("out_stored0"), sem("out_stored1")]

        x0_b = x0.rearrange("b (t p) d -> (b t) p d", p=P)
        out_b = out.rearrange("b (t p) d -> (b t) p d", p=P)

        def group_of(dram, g):
            return dram[bass.ds(g * GB, GB), :, :].rearrange("t p d -> p t d")

        def col(v):
            return v.rearrange("(c p) -> p c", p=P)

        def row_bc(v):
            return v.rearrange("(o n) -> o n", o=1).broadcast_to([P, v.shape[0]])

        NLOAD = 10
        JOBS = [(NCOMP, 0, 0, 0), (NCOMP, 1, NCOMP, 4), (P, 0, B * NCOMP, 8), (P, 1, B * NCOMP + P, 9)]
        ctx.enter_context(nc.allow_non_contiguous_dma(reason="biases and scales, a few hundred elements"))
        block = ctx.enter_context(nc.Block())

        @block.sync
        def _(sp):
            def load_rope_operands(lay):
                sp.dma_start(qk_sc[:, 0], q_scale[lay].rearrange("(o n) -> o n", o=1).broadcast_to([P, DH])).then_inc(small_loaded, 16)
                sp.dma_start(qk_sc[:, 1], k_scale[lay].rearrange("(o n) -> o n", o=1).broadcast_to([P, DH])).then_inc(small_loaded, 16)
                sp.dma_start(raw[:, 2, 0:BPB * 64], rope_base[:, 0]).then_inc(small_loaded, 16)
                sp.dma_start(pT[:].rearrange("p a n -> p (a n)"), rope_base[:, 1]).then_inc(small_loaded, 16)

            for g in range(2):
                sp.dma_start(x_in[:, g], group_of(x0_b, g)).then_inc(x_loaded[g], 16)
            for started in (l_copied, v_ready, win_add, x_attn, x_ffn, xnT_ps, xnT_ready, rows_ready, nT_ps, nT_lo, *out_stored):
                sp.sem_inc(started, 1)
            sp.wait_ge(rows_zero, 2)
            for b in range(B):
                sp.dma_start(wsg_sb[:, :, 32 * b:32 * b + 1], Ws.rearrange("(c p) n -> p c n", p=P)).then_inc(w_small, 16)
                sp.dma_start(wsg_sb[:, :, 32 * b + 1:32 * b + 4], Wg.rearrange("(c p) n -> p c n", p=P)).then_inc(w_small, 16)
                sp.dma_start(bsg_sb[32 * b:32 * b + 1, :], bs.rearrange("(p o) -> p o", o=1)).then_inc(w_small, 16)
                sp.dma_start(bsg_sb[32 * b + 1:32 * b + 4, :], bg.rearrange("(p o) -> p o", o=1)).then_inc(w_small, 16)
            for w_sb, w in ((wq_sb, Wq), (wk_sb, Wk), (wv_sb, Wv)):
                sp.dma_start(w_sb[:], w.rearrange("(c p) n -> p c n", p=P)).then_inc(w_loaded, 16)
            sp.dma_start(wo3_sb[:], Wo.rearrange("(c p) n -> p c n", p=P)).then_inc(w_loaded, 16)
            sp.dma_start(wc_sb[:], Wc.rearrange("(c p) n -> p c n", p=P)).then_inc(w_loaded, 16)
            for i, v in enumerate((bq, bk, bc)):
                sp.dma_start(bqkc_sb[:, i], col(v)).then_inc(w_loaded, 16)
            sp.dma_start(bv_bc[:], row_bc(bv)).then_inc(w_loaded, 16)
            sp.dma_start(bo_bc[:], row_bc(bo)).then_inc(w_loaded, 16)
            with sp.Fori(0, NG // 2 - 1) as u:
                for i in range(2):
                    sp.wait_ge(l_norm, u * (2 * GB) + (i + 1) * GB)
                    sp.dma_start(x_in[:, i], group_of(x0_b, u * 2 + 2 + i)).then_inc(x_loaded[i], 16)
            sp.dma_start(raw[:, 0:2], wqkv[0].rearrange("(c p) n -> p c n", p=P)).then_inc(raw_attn, 16)
            end_phase(sp, 1)
            end_phase(sp, 2)
            arrive(sp)
            load_rope_operands(0)
            sp.dma_start(x_in[:, 0], group_of(x0_b, 0)).then_inc(x0_loaded, 16)
            sp.wait_ge(x0_loaded, 16)
            sp.dma_start(x_in[:, 1], group_of(x0_b, 1)).then_inc(x0_loaded, 16)
            def move_group(g, i):
                sp.wait_ge(x_made, (g + 1) * GB)
                sp.dma_start(hs_attn[1:P, bass.ds(g * GB + g // GPB, GB), :],
                             x_sb[0:P - 1, bass.ds(g * GB, GB), P:D]).then_inc(hs_moved, 16)
                sp.dma_start(hs_attn[0:1, bass.ds(g * GB + g // GPB + 1, GB), :],
                             x_sb[P - 1:P, bass.ds(g * GB, GB), P:D]).then_inc(hs_moved, 16)
                sp.dma_start(group_of(x1_dram, g), x_in[:, i]).then_inc(x1_stored, 16)

            with sp.Fori(0, NG // 2 - 1) as u:
                for i in range(2):
                    g = u * 2 + i
                    move_group(g, i)
                    sp.wait_ge(x1_stored, 16 * (g + 1))
                    sp.wait_ge(x0_loaded, 16 * (g + 2))
                    sp.dma_start(x_in[:, i], group_of(x0_b, g + 2)).then_inc(x0_loaded, 16)
            move_group(NG - 2, 0)
            sp.wait_ge(x1_stored, 16 * (NG - 1))
            move_group(NG - 1, 1)
            sp.wait_ge(x1_stored, 16 * NG)
            sp.wait_ge(hs_moved, 32 * NG)
            await_phase(sp, 3)

            with sp.Fori(0, DEPTH) as lay:
                end_phase(sp, 4 + 4 * lay)
                sp.dma_start(wo_sb[:], wo[lay].rearrange("(c p) n -> p c n", p=P)).then_inc(wo_loaded, 16)
                sp.dma_start(ln_gb[:, 0], col(ln_g[lay])).then_inc(wo_loaded, 16)
                sp.dma_start(ln_gb[:, 1], col(ln_b[lay])).then_inc(wo_loaded, 16)
                for i in range(2):
                    sp.dma_start(b1_sb[0:FW, i, 0:FC - 1], b1[lay][i * HID:i * HID + (FC - 1) * FW].rearrange("(c p) -> p c", p=FW)).then_inc(wo_loaded, 16)
                    sp.dma_start(b1_sb[0:fw(FC - 1), i, FC - 1:FC], b1[lay][i * HID + (FC - 1) * FW:(i + 1) * HID].rearrange("(c p) -> p c", c=1)).then_inc(wo_loaded, 16)
                sp.dma_start(b2_sb[:], b2[lay].rearrange("(o n) -> o n", o=1).broadcast_to([P, D])).then_inc(wo_loaded, 16)
                sp.dma_start(raw[:, 0:2, 0:2 * HID], w1[lay].rearrange("(c p) n -> p c n", p=P)).then_inc(raw_ffn, 16)
                raw_w2 = raw[:, 2, :].rearrange("p (c n) -> p c n", n=D)
                sp.dma_start(raw_w2[0:FW, 0:FC - 1], w2[lay][0:(FC - 1) * FW, :].rearrange("(c p) n -> p c n", p=FW)).then_inc(raw_ffn, 16)
                sp.dma_start(raw_w2[0:fw(FC - 1), FC - 1], w2[lay][(FC - 1) * FW:HID, :]).then_inc(raw_ffn, 16)
                arrive(sp)
                for first, last in ((0, GB), (GB, NB)):
                    with sp.Fori(first, last) as t:
                        sp.wait_ge(x_attn, 1 + lay * NB + t + 1)
                        sp.dma_start(hs_ffn[1:P, t + t // BPB, :], x_sb[0:P - 1, t, P:D]).then_inc(hs_ffn_moved, 16)
                        sp.dma_start(hs_ffn[0:1, t + t // BPB + 1, :], x_sb[P - 1:P, t, P:D]).then_inc(hs_ffn_moved, 16)
                    if first == 0:
                        sp.wait_ge(hs_ffn_moved, 32 * (NB * lay + GB))
                        settle(sp)
                sp.wait_ge(hs_ffn_moved, 32 * NB * (lay + 1))
                settle(sp)
                sp.wait_ge(raw_ffn, 48 * (lay + 1))
                settle(sp)
                await_phase(sp, 5 + 4 * lay)
                end_phase(sp, 6 + 4 * lay)
                sp.dma_start(raw[:, 0:2], wqkv[(lay + 1) % DEPTH].rearrange("(c p) n -> p c n", p=P)).then_inc(raw_attn, 16)
                load_rope_operands((lay + 1) % DEPTH)
                arrive(sp)
                with sp.Fori(0, NG) as g:
                    sp.wait_ge(x_ffn, 1 + (lay * NG + g + 1) * 2)
                    sp.dma_start(hs_attn[1:P, bass.ds(g * GB + g // GPB, GB), :],
                                 x_sb[0:P - 1, bass.ds(g * GB, GB), P:D]).then_inc(hs_attn_moved, 16)
                    sp.dma_start(hs_attn[0:1, bass.ds(g * GB + g // GPB + 1, GB), :],
                                 x_sb[P - 1:P, bass.ds(g * GB, GB), P:D]).then_inc(hs_attn_moved, 16)
                sp.wait_ge(hs_attn_moved, 32 * NG * (lay + 1))
                settle(sp)
                sp.wait_ge(raw_attn, 16 * (lay + 2))
                settle(sp)
                sp.wait_ge(small_loaded, 64 * (lay + 2))
                settle(sp)
                await_phase(sp, 7 + 4 * lay)

            for i in range(2):
                sp.dma_start(f_x1[:, i], group_of(x1_dram, i)).then_inc(f_x1_loaded[i], 16)
            with sp.Fori(0, NG // 2 - 1) as u:
                for i in range(2):
                    g = u * 2 + i
                    sp.wait_ge(f_sum, g + 1)
                    sp.dma_start(group_of(out_b, g), f_y[:, i]).then_inc(out_stored[i], 16)
                    sp.dma_start(f_x1[:, i], group_of(x1_dram, g + 2)).then_inc(f_x1_loaded[i], 16)
            for i in range(2):
                g = NG - 2 + i
                sp.wait_ge(f_sum, g + 1)
                sp.dma_start(group_of(out_b, g), f_y[:, i]).then_inc(out_stored[i], 16)
            for i in range(2):
                sp.wait_ge(out_stored[i], 1 + 16 * (NG // 2))

        @block.gpsimd
        def _(pool):
            pool.memset(ident[:], 0.0).then_inc(sc_made, 1)
            pool.memset(mask_tab[:, 0], BIG).then_inc(sc_made, 1)
            pool.memset(mask_tab[:, 1], 0.0).then_inc(sc_made, 1)
            pool.memset(mask_even[:], 0.0).then_inc(sc_made, 1)
            pool.memset(mask_win[:], 0.0).then_inc(sc_made, 1)
            pool.memset(neg_half[:], -0.5).then_inc(sc_made, 1)
            pool.memset(hs_attn[:], 0.0).then_inc(sc_made, 1)
            pool.memset(hs_ffn[:], 0.0).then_inc(sc_made, 1)
            pool.memset(rows[:], 0.0).then_inc(rows_zero, 1)
            pool.memset(wsg_sb[:], 0.0).then_inc(rows_zero, 1)
            pool.memset(warm[:], 1.0).then_inc(sc_made, 1)
            pool.memset(zero[:], 0.0).then_inc(sc_made, 1)
            pool.iota(iota1[:], pattern=[[1, P]], base=1, channel_multiplier=0,
                      allow_small_or_imprecise_dtypes=True).then_inc(sc_made, 1)
            pool.wait_ge(sc_made, 11)
            pool.affine_select(out=ident[:], in_=ident[:], compare_op=ALU.not_equal, fill=1.0, base=0,
                               pattern=[[-1, P]], channel_multiplier=1).then_inc(sc_made, 1)
            pool.affine_select(out=mask_tab[:, 1], in_=mask_tab[:, 1], compare_op=ALU.is_ge, fill=BIG, base=0,
                               pattern=[[1, P]], channel_multiplier=-1).then_inc(sc_made, 1)
            pool.affine_select(out=mask_even[:, 0], in_=mask_even[:, 0], compare_op=ALU.is_ge, fill=BIG, base=0,
                               pattern=[[-1, P]], channel_multiplier=1).then_inc(sc_made, 1)
            pool.wait_ge(sc_made, 14)
            pool.affine_select(out=mask_win[0:WIN], in_=mask_win[0:WIN], compare_op=ALU.is_gt, fill=-BIG, base=WIN,
                               pattern=[[-1, WK]], channel_multiplier=0).then_inc(sc_made, 1)
            pool.wait_ge(sc_made, 15)
            pool.affine_select(out=mask_win[WIN:P], in_=mask_win[WIN:P], compare_op=ALU.is_ge, fill=-BIG, base=-WIN // 2,
                               pattern=[[1, WK]], channel_multiplier=0).then_inc(sc_made, 1)
            pool.wait_ge(sc_made, 16)
            pool.tensor_copy(mask_odd[:, 0], mask_tab[:, 1]).then_inc(sc_made, 1)
            pool.tensor_copy(mask_odd[:, 1], mask_even[:, 0]).then_inc(sc_made, 1)
            pool.wait_ge(sc_made, 18)
            pool.tensor_copy(mask_even[:, 1], mask_tab[:, 1]).then_inc(consts_ready, 1)

            def inverse_root(var, out_ap, eps, ready, n_ready, stepped, n_step, done, width):
                pool.wait_ge(ready, n_ready)
                settle(pool)
                pool.tensor_scalar(out_ap, var, eps, None, ALU.add).then_inc(stepped, 1)
                pool.wait_ge(stepped, n_step)
                settle(pool)
                pool.tensor_tensor(out_ap, out_ap, neg_half[:, 0:width], ALU.pow).then_inc(done, 1)

            with pool.Fori(0, NG // 2) as u:
                for i in range(2):
                    g = u * 2 + i
                    inverse_root(l_mv[:, i, :, 1], l_rstd[:, i], 1e-5, l_stats, (g + 1) * GB, l_eps, g + 1, l_rs, GB)
            end_phase(pool, 1)
            for b in range(B):
                pool.wait_ge(sel_used, (b + 1) * BPB)
                pool.tensor_tensor(x_sb[:, b * BPB:(b + 1) * BPB, :], x_sb[:, b * BPB:(b + 1) * BPB, :],
                                   bo_bc[:, None, :].broadcast_to([P, BPB, D]), ALU.add).then_inc(bo_added, 1)
            end_phase(pool, 2)

            def double_norm_scale(b):
                pool.wait_ge(m_aggr, b + 1)
                settle(pool)
                var = m_mv[:, 1:2]
                pool.tensor_scalar(m_t[:, 0:1], var, 0.25, 1e-6, ALU.mult, ALU.add).then_inc(m_step, 1)
                pool.tensor_scalar(m_t[:, 1:2], var, 0.25, None, ALU.mult).then_inc(m_step, 1)
                pool.wait_ge(m_step, 7 * b + 2)
                pool.tensor_tensor(m_t[:, 0:1], m_t[:, 0:1], neg_half[:, 0:1], ALU.pow).then_inc(m_step, 1)
                pool.wait_ge(m_step, 7 * b + 3)
                pool.tensor_tensor(m_t[:, 2:3], m_t[:, 1:2], m_t[:, 0:1], ALU.mult).then_inc(m_step, 1)
                pool.wait_ge(m_step, 7 * b + 4)
                pool.tensor_tensor(m_t[:, 3:4], m_t[:, 2:3], m_t[:, 0:1], ALU.mult).then_inc(m_step, 1)
                pool.wait_ge(m_step, 7 * b + 5)
                settle(pool)
                pool.tensor_scalar(m_t[:, 4:5], m_t[:, 3:4], 1e-5, 4.0, ALU.add, ALU.mult).then_inc(m_step, 1)
                pool.wait_ge(m_step, 7 * b + 6)
                pool.tensor_tensor(m_t[:, 5:6], m_t[:, 4:5], neg_half[:, 0:1], ALU.pow).then_inc(m_step, 1)
                pool.wait_ge(m_step, 7 * b + 7)
                pool.tensor_tensor(m_scale[:], m_t[:, 5:6], m_t[:, 0:1], ALU.mult).then_inc(m_scaled, 1)

            def x1_norm_root(b):
                inverse_root(f_mv1[:, 1:2], f_r[:], 1e-5, x1_aggr, b + 1, x1_step, b + 1, x1_root, 1)

            double_norm_scale(0)
            double_norm_scale(1)
            with pool.Fori(0, NB - 2) as b:
                x1_norm_root(b)
                double_norm_scale(b + 2)
            arrive(pool)
            x1_norm_root(NB - 2)
            x1_norm_root(NB - 1)
            await_phase(pool, 3)

            with pool.Fori(0, DEPTH) as lay:
                pool.wait_ge(small_loaded, 64 * (lay + 1))
                settle(pool)
                pool.tensor_scalar(sc_x[:, 0, 0], qk_sc[:, 0], -QK_SCALE, None, ALU.mult).then_inc(sc_made, 1)
                pool.tensor_copy(sc_x[:, 0, 1], qk_sc[:, 1]).then_inc(sc_made, 1)
                for i, s in ((0, QK_SCALE), (1, -1.0)):
                    pool.tensor_scalar(sc_x[:, 1, i, 0:32], qk_sc[:, i, 32:64], s, None, ALU.mult).then_inc(sc_made, 1)
                    pool.tensor_scalar(sc_x[:, 1, i, 32:64], qk_sc[:, i, 0:32], -s, None, ALU.mult).then_inc(sc_made, 1)
                pool.wait_ge(sc_made, 18 + 6 * (lay + 1))
                sn = pT[:].rearrange("p a (t k d) -> p (a t) k d", k=2, d=32)
                for i, h in ((0, 0), (0, 1), (1, 0)):
                    pool.tensor_tensor(rope[:, :, 1, i, 32 * h:32 * h + 32], sn[:, :, i, :],
                                       sc_x[:, 1, i, 32 * h:32 * h + 32][:, None, :].broadcast_to([P, BPB, 32]), ALU.mult)
                end_phase(pool, 4 + 4 * lay)

                def stage_h(t):
                    pool.tensor_copy(h_in[:, 0], x_sb[:, t, 0:P]).then_inc(h_staged, 1)
                    pool.tensor_copy(h_in[:, 1], hs_attn[:, t + t // BPB, :]).then_inc(h_staged, 1)

                def front(f):
                    for which in range(2):
                        part = slice(which * HEADS, (which + 1) * HEADS)
                        pool.wait_ge(ss_floor[which], f + 1)
                        settle(pool)
                        pool.tensor_tensor(rnorm[:, part], sumsq[:, part], neg_half[:, part], ALU.pow).then_inc(r_ready[which], 1)
                        if which == 0:
                            pool.wait_ge(rotated[0], 2 * f + 2)
                            pool.tensor_tensor(qk_cos[:, 0], qk_cos[:, 0], qk_sin[:, 0], ALU.add).then_inc(z_ready[0], 1)

                f0 = lay * (NB + 1)
                stage_h(0)
                pool.tensor_copy(mask_even[:, 1], mask_tab[:, 0]).then_inc(mask_set, 1)
                front(f0)
                for t in (1, 2):
                    pool.wait_ge(hT_ps, f0 + lay + t)
                    settle(pool)
                    stage_h(t)
                with pool.Fori(0, NB // 2) as u:
                    for i in range(2):
                        t = u * 2 + i
                        front(f0 + t + 1)
                        if i == 0:
                            pool.wait_ge(masked, (lay * NB + t + 1) * HEADS + 2 * lay)
                            settle(pool)
                            pool.tensor_copy(mask_even[:, 1], mask_tab[:, ((u + 1) % (BPB // 2) + (BPB // 2 - 1)) // (BPB // 2)]).then_inc(mask_set, 1)
                        pool.wait_ge(hT_ps, f0 + lay + t + 3)
                        pool.wait_ge(x_attn, 1 + lay * NB + t)
                        settle(pool)
                        stage_h((t + 3) % NB)
                end_phase(pool, 5 + 4 * lay)

                def norm_lo(n, half):
                    for c in range(DC):
                        pool.wait_ge(nT_full, 2 * n + c + 1)
                        pool.wait_ge(nT_hi, 2 * n + c + 1)
                        settle(pool)
                        pool.tensor_tensor(h_lo[:, half, c], h_full[:, c], h_hi[:, half, c], ALU.subtract).then_inc(nT_lo, 1)

                n0 = lay * (NG + 1)
                pool.wait_ge(split_hi, SPLITS * lay + DC + 2)
                settle(pool)
                pool.tensor_tensor(w1_lo[:, 1], raw[:, 1, 0:2 * HID], w1_hi[:, 1], ALU.subtract)
                inverse_root(mv[:, :, 1], rstd[:], 1e-5, n_aggr, (n0 + 1) * GB, n_eps, n0 + 1, n_rs, GB)
                norm_lo(n0, 0)
                end_phase(pool, 6 + 4 * lay)
                with pool.Fori(0, NG // 2) as u:
                    for i in range(2):
                        g = u * 2 + i
                        k = lay * NG + g
                        pool.wait_ge(n_norm, 8 * (n0 + g + 1))
                        settle(pool)
                        pool.tensor_tensor(x_sb[:, bass.ds(g * GB, GB), :], x_sb[:, bass.ds(g * GB, GB), :],
                                           b2_sb[:, None, :].broadcast_to([P, GB, D]), ALU.add).then_inc(b2_added, 1)
                        for j in range(FC):
                            if j == 1:
                                inverse_root(mv[:, :, 1], rstd[:], 1e-5, n_aggr, (n0 + g + 2) * GB, n_eps, n0 + g + 2, n_rs, GB)
                            pool.wait_ge(act_hi_ready, FC * k + j + 1)
                            if j >= 3:
                                pool.wait_ge(w2_used, FC * k + j - 2)
                            settle(pool)
                            w = fw(j)
                            pool.tensor_tensor(act_lo[0:w, j % 3], act_full[0:w, j % 2], act_hi[0:w, j % 3], ALU.subtract).then_inc(act_lo_ready, 1)
                        norm_lo(n0 + g + 1, 1 - i)
                end_phase(pool, 7 + 4 * lay)

            def last_root(g, i):
                inverse_root(f_mv[:, i, :, 1], f_rstd[:, i], 1e-5, f_stats, (g + 1) * GB, f_eps, g + 1, f_rs, GB)

            def last_sum(u, i):
                pool.wait_ge(f_norm, (u * 2 + i + 1) * GB)
                pool.wait_ge(f_x1_loaded[i], 16 * (u + 1))
                settle(pool)
                pool.tensor_tensor(f_y[:, i], f_y[:, i], f_x1[:, i], ALU.add).then_inc(f_sum, 1)

            last_root(0, 0)
            with pool.Fori(0, NG // 2 - 1) as u:
                last_root(u * 2 + 1, 1)
                last_sum(u, 0)
                last_root(u * 2 + 2, 0)
                last_sum(u, 1)
            last_root(NG - 1, 1)
            last_sum(NG // 2 - 1, 0)
            last_sum(NG // 2 - 1, 1)

        @block.scalar
        def _(act):
            act.wait_ge(consts_ready, 1)
            act.activation(warm[:], warm[:], ACT.Exp).then_inc(gate_exp, 1)
            for b in range(B):
                with act.Fori(0, GPB) as gg:
                    g = gg + b * GPB
                    for c in range(DC):
                        act.wait_ge(xnT_ps, 1 + 2 * g + c + 1)
                        settle(act)
                        act.activation(xnT[:, c, bass.ds(g * GT, GT)], bank[:, c], ACT.Copy).then_inc(xnT_ready, 1)
                    act.wait_ge(rows_zero, 2)
                    act.wait_ge(w_small, 16 * 8)
                    act.wait_ge(rows_ps, g + 1)
                    settle(act)
                    act.activation(rows[32 * b:32 * b + 4, bass.ds(gg * GT, GT)], bank[32 * b:32 * b + 4, 2],
                                   ACT.Identity, bias=bsg_sb[32 * b:32 * b + 4, :]).then_inc(rows_ready, 1)
            end_phase(act, 1)

            act.wait_ge(row_t_ready, 1)
            act.activation(gate[:, :, 0], turned[:, :, 1:4], ACT.Exp, scale=-1.0).then_inc(gate_exp, 1)
            act.activation(gate[:, :, 1], turned[:, :, 33:36], ACT.Exp, scale=-1.0).then_inc(gate_exp, 1)
            act.wait_ge(w_loaded, 16 * NLOAD)
            for job, (T, b, at, n0) in enumerate(JOBS):
                act.wait_ge(tok_ps, job + 1)
                for m in range(DC):
                    if T == NCOMP:
                        act.activation(tokT[:, m, 0:T], bank[:, m, 0:T], ACT.Identity, bias=bqkc_sb[:, 2, m:m + 1]).then_inc(tok_ready, 1)
                    else:
                        act.activation(tokT[:, m, 0:T], bank[:, m, 0:T], ACT.Copy).then_inc(tok_ready, 1)
                for i, dst in enumerate((qTc, kTc)):
                    for m in range(DC):
                        act.wait_ge(com_qk_ps, 4 * job + 2 * i + m + 1)
                        act.activation(dst[:, m, 0:T], bank[:, 2 + 2 * i + m, 0:T], ACT.Identity, bias=bqkc_sb[:, i, m:m + 1]).then_inc(com_qk, 1)
                for qb in range(T // P):
                    act.wait_ge(com_nm, n0 + qb + 1)
                    act.activation(pc[:, 0:T], bank[:, 6, 0:T], ACT.Exp, bias=c_max[:, 1:2], scale=SCALE, accum_out=c_max[:, 2:3]).then_inc(com_e, 1)
                    act.wait_ge(com_pt_ps, n0 + qb + 1)
                    act.activation(pTc[:, 0:T // P, qb * P:(qb + 1) * P], bank[:, 7, 0:T].rearrange("p (k q) -> p k q", q=P), ACT.Copy).then_inc(com_pt, 1)
                act.wait_ge(com_c_ps, job + 1)
                act.activation(cT[:, :, at:at + T], bank[:, 0:2, 0:T], ACT.Copy).then_inc(com_c, 1)
            end_phase(act, 2)

            def token(j):
                return (j % NB) // BPB * N + (j % BPB) * WIN

            def win_front(j):
                if type(j) is not int or j:
                    act.wait_ge(win_v_ps, j)
                settle(act)
                act.activation(xw[:], xnT[:, :, bass.ds(token(j), WK)], ACT.Copy).then_inc(win_x, 1)

            def win_qk(j):
                act.wait_ge(win_q_ps, j + 1)
                if type(j) is not int or j:
                    act.wait_ge(win_s, j)
                for m in range(DC):
                    for w in range(2):
                        act.activation(qTw[:, m, w, :], bank[:, 0, m * WK + w * WIN // 2:m * WK + w * WIN // 2 + WIN],
                                       ACT.Identity, bias=bqkc_sb[:, 0, m:m + 1]).then_inc(win_q, 1)
                act.wait_ge(win_k_ps, j + 1)
                for m in range(DC):
                    act.activation(kTw[:, m], bank[:, 1, m * WK:(m + 1) * WK],
                                   ACT.Identity, bias=bqkc_sb[:, 1, m:m + 1]).then_inc(win_k, 1)

            def win_exp(j):
                act.wait_ge(win_m, j + 1)
                act.activation(pw[:], pw[:], ACT.Exp, bias=w_max[:, 0:1], scale=-1.0,
                               accum_out=w_max[:, 2:3]).then_inc(win_e, 1)

            win_qk(0)
            win_front(0)
            win_exp(0)
            win_qk(1)
            win_front(1)
            with act.Fori(0, NB) as j:
                act.wait_ge(win_pt_ps, j + 1)
                act.activation(pTw[0:WK, :], bank[0:WK, 4, 0:P], ACT.Copy).then_inc(win_pt, 1)
                act.wait_ge(win_c_ps, j + 1)
                act.activation(cTw[:], bank[:, 5, 0:2 * P].rearrange("p (m q) -> p m q", m=DC), ACT.Copy).then_inc(win_c, 1)
                win_exp(j + 1)
                win_front(j + 2)
                win_qk(j + 2)
            end_phase(act, 3)

            act.wait_ge(raw_attn, 16)
            for c in range(DC):
                act.activation(wqkv_hi[:, c], raw[:, c], ACT.Copy).then_inc(split_hi, 1)

            with act.Fori(0, DEPTH) as lay:
                act.wait_ge(x_made, NB)
                act.activation(qT[:], zero[:, 0:1, None, None].broadcast_to([P, HEADS // 2, 2, P]), ACT.Copy).then_inc(kv_zero, 1)
                act.activation(kT[:, :, 1], zero[:, 0:1, None].broadcast_to([P, HEADS // 2, P]), ACT.Copy).then_inc(kv_zero, 1)
                act.activation(v_sb[:, 1], zero[:].broadcast_to([P, INNER]), ACT.Copy).then_inc(kv_zero, 1)
                end_phase(act, 4 + 4 * lay)

                def hi(g):
                    act.wait_ge(hT_ps, g + 1)
                    act.activation(hT_hi[:], bank[:, 5, 0:2 * P].rearrange("p (c t) -> p c t", c=DC), ACT.Copy).then_inc(hT_hi_ready, 1)

                def square(f, which):
                    act.wait_ge(qk_raw[which], f + 1)
                    act.activation(qk_sq[:, which], bank[:, which], ACT.Square).then_inc(squares[which], 1)

                def q_out(f):
                    act.wait_ge(qkT_ps[0], f + 1)
                    act.activation(qT[DH:P, :, 1, :], bank[DH:P, 0].rearrange("p (c t) -> p c t", t=P), ACT.Copy).then_inc(q_odd, 1)

                def v_out(f, half):
                    act.wait_ge(v_raw, f + 1)
                    act.activation(v_sb[:, half], bank[:, 2], ACT.Copy).then_inc(v_ready, 1)

                def exponent(k, h):
                    act.wait_ge(masked, HEADS * k + 2 * lay + h + 1)
                    act.activation(prob[:, h], prob[:, h], ACT.Exp, bias=neg_max[:, h:h + 1], scale=-1.0,
                                   accum_out=psums[:, h:h + 1]).then_inc(exped, 1)

                def weigh_odd(k, h):
                    act.wait_ge(inverted, HEADS * k + h + 1)
                    act.activation(prob[:, h], prob[:, h], ACT.Copy, scale=pinv[:, h:h + 1]).then_inc(p_odd, 1)

                def probs_out(k, j):
                    act.wait_ge(pt_ps, 4 * k + j + 1)
                    if j >= 2:
                        act.wait_ge(pv_done, 4 * k + j - 1)
                    act.activation(pT[:, j % 2], bank[:, 5 + j % 2], ACT.Copy).then_inc(pt_ready, 1)

                f0 = lay * (NB + 1)
                hi(f0 + lay)
                square(f0, 0)
                square(f0, 1)
                v_out(f0, 0)
                hi(f0 + lay + 1)
                act.wait_ge(kv_zero, 3 * lay + 3)
                q_out(f0)
                with act.Fori(0, NB // 2) as u:
                    for i in range(2):
                        k = lay * NB + u * 2 + i
                        f = f0 + u * 2 + i + 1
                        for h in range(4):
                            exponent(k, h)
                        square(f, 0)
                        weigh_odd(k, 1)
                        exponent(k, 4)
                        exponent(k, 5)
                        square(f, 1)
                        weigh_odd(k, 3)
                        probs_out(k, 0)
                        probs_out(k, 1)
                        exponent(k, 6)
                        exponent(k, 7)
                        weigh_odd(k, 5)
                        weigh_odd(k, 7)
                        probs_out(k, 2)
                        probs_out(k, 3)
                        hi(f + lay + 1)
                        act.wait_ge(pv_done, 4 * k + 4)
                        act.activation(oT[:], bank[:, 7].rearrange("p (c t) -> p c t", t=P), ACT.Copy).then_inc(ot_ready, 1)
                        q_out(f)
                        v_out(f, 1 - i)
                arrive(act)
                act.activation(warm[:], warm[:], ACT.Gelu).then_inc(gate_exp, 1)
                act.wait_ge(raw_ffn, 48 * (lay + 1))
                for c in range(DC):
                    act.activation(w1_hi[:, c], raw[:, c, 0:2 * HID], ACT.Copy).then_inc(split_hi, 1)
                raw_w2 = raw[:, 2, :].rearrange("p (c n) -> p c n", n=D)
                act.activation(w2_hi[0:FW, 0:FC - 1], raw_w2[0:FW, 0:FC - 1], ACT.Copy).then_inc(split_hi, 1)
                act.activation(w2_hi[0:fw(FC - 1), FC - 1], raw_w2[0:fw(FC - 1), FC - 1], ACT.Copy).then_inc(split_hi, 1)
                await_phase(act, 5 + 4 * lay)


                def norm_hi(n, half):
                    for c in range(DC):
                        act.wait_ge(nT_ps, 1 + n + 1)
                        act.activation(h_hi[:, half, c], bank[:, 6 + c], ACT.Identity, bias=ln_gb[:, 1, c:c + 1],
                                       scale=ln_gb[:, 0, c:c + 1]).then_inc(nT_hi, 1)

                n0 = lay * (NG + 1)
                act.wait_ge(wo_loaded, 16 * 8 * (lay + 1))
                norm_hi(n0, 0)
                end_phase(act, 6 + 4 * lay)
                with act.Fori(0, NG // 2) as u:
                    for i in range(2):
                        k = lay * NG + u * 2 + i
                        for j in range(FC):
                            w = fw(j)
                            act.wait_ge(g_ps, FC * k + j + 1)
                            if j >= 2:
                                act.wait_ge(act_ready, FC * k + j - 1)
                            act.activation(gelu_sb[0:w, j % 2], bank[0:w, j % 2], ACT.Gelu, bias=b1_sb[0:w, 1, j:j + 1]).then_inc(g_ready, 1)
                            if j == 4:
                                norm_hi(n0 + u * 2 + i + 1, 1 - i)
                            if i == 0 and j == 5:
                                act.wait_ge(raw_attn, 16 * (lay + 2))
                                act.activation(wqkv_hi[:, :, bass.ds(u * SHARE, SHARE)], raw[:, 0:2, bass.ds(u * SHARE, SHARE)],
                                               ACT.Copy).then_inc(split_hi, 1)
                act.activation(warm[:], warm[:], ACT.Exp).then_inc(gate_exp, 1)
                end_phase(act, 7 + 4 * lay)

        @block.tensor
        def _(pe):
            pe.wait_ge(consts_ready, 1)
            pe.wait_ge(w_small, 16 * 8)
            for b in range(B):
                with pe.Fori(0, GPB) as gg:
                    g = gg + b * GPB
                    pe.wait_ge(l_norm, (g + 1) * GB)
                    for c in range(DC):
                        if c == 0:
                            pe.wait_ge(xnT_ready, 1 + 2 * g)
                        for i in range(GB):
                            tr = pe.transpose(bank[:, c, i * P:(i + 1) * P], xn_st[:, i, c * P:(c + 1) * P], ident[:])
                        tr.then_inc(xnT_ps, 1)
                    pe.wait_ge(xnT_ready, 1 + 2 * g + 2)
                    pe.wait_ge(rows_ready, 1 + g)
                    for c in range(DC):
                        mm = pe.matmul(bank[0:36, 2], wsg_sb[:, c], xnT[:, c, bass.ds(g * GT, GT)],
                                       start=(c == 0), stop=(c == DC - 1))
                    mm.then_inc(rows_ps, 1)
            end_phase(pe, 1)

            for c in range(BPB):
                tr = pe.transpose(bank[:, 6 + c // 8, (c % 8) * 64:(c % 8) * 64 + 64], rows[:, c * P:(c + 1) * P], ident[0:64, 0:64])
            tr.then_inc(row_t_ps, 1)

            pe.wait_ge(w_loaded, 16 * NLOAD)

            def attend(job, T, at, n0):
                pe.wait_ge(tok_ready, 2 * (job + 1))
                for i, w_sb in enumerate((wq_sb, wk_sb)):
                    for m in range(DC):
                        for c in range(DC):
                            mm = pe.matmul(bank[:, 2 + 2 * i + m, 0:T], w_sb[:, c, m * P:(m + 1) * P], tokT[:, c, 0:T], start=(c == 0), stop=(c == DC - 1))
                        mm.then_inc(com_qk_ps, 1)
                for kb in range(T // P):
                    for c in range(DC):
                        mm = pe.matmul(bank[:, kb // 2, (kb % 2) * D:(kb % 2 + 1) * D], tokT[:, c, kb * P:(kb + 1) * P], wv_sb[:, c],
                                       start=(c == 0), stop=(c == DC - 1))
                mm.then_inc(com_v_ps, 1)
                pe.wait_ge(com_qk, 4 * (job + 1))
                for qb in range(T // P):
                    n = n0 + qb
                    pe.wait_ge(com_e, n)
                    for c in range(DC):
                        mm = pe.matmul(bank[:, 6, 0:T], qTc[:, c, qb * P:(qb + 1) * P], kTc[:, c, 0:T], start=(c == 0), stop=(c == DC - 1))
                    mm.then_inc(com_s, 1)
                    pe.wait_ge(com_p, n + 1)
                    pe.wait_ge(com_pt, n)
                    for kb in range(T // P):
                        tr = pe.transpose(bank[:, 7, kb * P:(kb + 1) * P], pc[:, kb * P:(kb + 1) * P], ident[:])
                    tr.then_inc(com_pt_ps, 1)
                pe.wait_ge(com_v, job + 1)
                pe.wait_ge(com_pt, n0 + T // P)
                for m in range(DC):
                    for kb in range(T // P):
                        mm = pe.matmul(bank[:, m, 0:T], vc[:, kb, m * P:(m + 1) * P], pTc[:, kb, 0:T], start=(kb == 0), stop=(kb == T // P - 1))
                mm.then_inc(com_c_ps, 1)

            for job, (T, b, at, n0) in enumerate(JOBS):
                if job:
                    pe.wait_ge(com_c, job)
                if T == NCOMP:
                    for m in range(DC):
                        n = 0
                        for r in range(RATIO):
                            for c in range(DC):
                                xr = xnT[:, c, b * N:(b + 1) * N].rearrange("p (i r) -> p r i", r=RATIO)[:, r]
                                mm = pe.matmul(bank[:, m], wc_sb[:, r * DC + c, m * P:(m + 1) * P], xr, start=(n == 0), stop=(n == RATIO * DC - 1))
                                n += 1
                    mm.then_inc(tok_ps, 1)
                else:
                    if b == 0:
                        pe.wait_ge(topk_step, 2 * ROUNDS + 4)
                        pe.wait_ge(com_e, n0)
                        pe.wait_ge(com_pt, n0)
                        for c in range(BPB):
                            tr = pe.transpose(bank[:, 6 + c // 8, (c % 8) * 64:(c % 8) * 64 + 64], place_row[:, c * P:(c + 1) * P], ident[0:64, 0:64])
                        tr.then_inc(pos_ps, 1)
                    for c in range(BPB):
                        n = b * BPB + c
                        pe.wait_ge(sel_made, n + 1)
                        for m in range(DC):
                            mm = pe.matmul(bank[:, m, 0:P], x_sb[:, n, m * P:(m + 1) * P], sel_m[:, n % 2], start=(c == 0), stop=(c == BPB - 1))
                        mm.then_inc(sel_used, 1)
                    pe.drain().then_inc(tok_ps, 1)
                    if b == 0:
                        pe.wait_ge(pos_ready, 1)
                attend(job, T, at, n0)
            pe.wait_ge(com_c, len(JOBS))
            for n in range(B * (NCOMP // P)):
                b, qb = divmod(n, NCOMP // P)
                if n:
                    pe.wait_ge(com_add, n)
                terms = [(cT[:, m, n * P:(n + 1) * P], m) for m in range(DC)]
                if qb == 0:
                    at = B * NCOMP + b * P
                    terms += [(cT[:, m, at:at + P], DC + m) for m in range(DC)]
                for i, (c_ap, row) in enumerate(terms):
                    mm = pe.matmul(bank[:, 6, 0:D], c_ap, wo3_sb[:, row], start=(i == 0), stop=(i == len(terms) - 1))
                mm.then_inc(com_o, 1)
            end_phase(pe, 2)

            def token(j):
                return (j % NB) // BPB * N + (j % BPB) * WIN

            def win_qk(j):
                for i, w_sb in enumerate((wq_sb, wk_sb)):
                    for m in range(DC):
                        for c in range(DC):
                            mm = pe.matmul(bank[:, i, m * WK:(m + 1) * WK], w_sb[:, c, m * P:(m + 1) * P], xnT[:, c, bass.ds(token(j), WK)],
                                           start=(c == 0), stop=(c == DC - 1))
                    mm.then_inc((win_q_ps, win_k_ps)[i], 1)

            def win_values(j, c):
                if c == 0:
                    pe.wait_ge(win_x, j + 1)
                    if type(j) is not int or j:
                        pe.wait_ge(win_v, j)
                mm = pe.matmul(bank[0:WK, 2, 0:D], xw[:, c], wv_sb[:, c], start=(c == 0), stop=(c == DC - 1))
                if c == DC - 1:
                    mm.then_inc(win_v_ps, 1)

            def win_scores(j):
                pe.wait_ge(win_q, 4 * j + 4)
                pe.wait_ge(win_k, 2 * j + 2)
                for m in range(DC):
                    mm = pe.matmul(bank[:, 3, 0:WK], qTw[:, m].rearrange("p a b -> p (a b)"), kTw[:, m], start=(m == 0), stop=(m == DC - 1))
                mm.then_inc(win_s, 1)

            win_qk(0)
            win_values(0, 0)
            win_values(0, 1)
            win_scores(0)
            win_qk(1)
            with pe.Fori(0, NB) as j:
                pe.wait_ge(win_p, j + 1)
                pe.transpose(bank[0:WK, 4, 0:P], pw[:], ident[:]).then_inc(win_pt_ps, 1)
                win_values(j + 1, 0)
                pe.wait_ge(win_pt, j + 1)
                for m in range(DC):
                    mm = pe.matmul(bank[:, 5, m * P:(m + 1) * P], vw[0:WK, m * P:(m + 1) * P], pTw[0:WK, :], start=True, stop=True)
                mm.then_inc(win_c_ps, 1)
                win_values(j + 1, 1)
                win_scores(j + 1)
                win_qk(j + 2)
                pe.wait_ge(win_c, j + 1)
                pe.wait_ge(win_add, 1 + j)
                for m in range(DC):
                    mm = pe.matmul(bank[:, 6, 0:D], cTw[:, m], wo3_sb[:, 2 * DC + m], start=(m == 0), stop=(m == DC - 1))
                mm.then_inc(win_o, 1)
            end_phase(pe, 3)

            with pe.Fori(0, DEPTH) as lay:
                end_phase(pe, 4 + 4 * lay)

                def transposes(g):
                    pe.wait_ge(h_staged, 2 * (g + lay) + 2)
                    for c in range(DC):
                        tr = pe.transpose(bank[:, 5, c * P:(c + 1) * P], h_in[:, c], ident[:])
                    tr.then_inc(hT_ps, 1)

                def project(f, s):
                    to, c = divmod(s, 2)
                    if s == 0:
                        pe.wait_ge(hT_hi_ready, f + lay + 1)
                        pe.wait_ge(hT_lo_ready, f + lay + 1)
                    if s == 4:
                        pe.wait_ge(v_ready, 1 + f)
                    cols = slice(to * INNER, (to + 1) * INNER)
                    pe.matmul(bank[:, to], hT_hi[:, c], wqkv_hi[:, c, cols], start=(c == 0), stop=False)
                    pe.matmul(bank[:, to], hT_hi[:, c], wqkv_lo[:, c, cols], start=False, stop=False)
                    mm = pe.matmul(bank[:, to], hT_lo[:, c], wqkv_hi[:, c, cols], start=False, stop=(c == 1))
                    if s in (1, 3):
                        mm.then_inc(qk_raw[to], 1)
                    if s == 5:
                        mm.then_inc(v_raw, 1)

                def turn_qk(f, which):
                    pe.wait_ge(qk_ready[which], f + 1)
                    for c in range(HEADS // 2):
                        tr = pe.transpose(bank[:, which, c * P:(c + 1) * P], qk_cos[:, which, c * P:(c + 1) * P], ident[:])
                    tr.then_inc(qkT_ps[which], 1)

                def scores(k, j):
                    if j >= 2:
                        pe.wait_ge(masked, HEADS * k + 2 * lay + 2 * j - 2)
                    for e in range(2):
                        mm = pe.matmul(bank[:, 3 + j % 2, e * 2 * P:(e + 1) * 2 * P], qT[:, j, e],
                                       kT[:, j].rearrange("p a b -> p (a b)"), start=True, stop=True)
                    mm.then_inc(s_ready, 1)

                def project_out(k, c):
                    mm = pe.matmul(bank[:, 6, 0:D], oT[:, c], wo_sb[:, c], start=(c == 0), stop=(c == INNER // P - 1))
                    if c == INNER // P - 1:
                        mm.then_inc(wo_ps, 1)

                def turn_probs(k, j):
                    if j == 1:
                        pe.wait_ge(x_attn, 1 + k)
                    if j >= 2:
                        pe.wait_ge(pt_ready, 4 * k + j - 1)
                    for h in (2 * j, 2 * j + 1):
                        pe.wait_ge((p_even, p_odd)[h % 2], HEADS // 2 * k + j + 1)
                        for c in range(2):
                            tr = pe.transpose(bank[:, 5 + j % 2, ((h % 2) * 2 + c) * P:((h % 2) * 2 + c + 1) * P], prob[:, h, c], ident[:])
                    tr.then_inc(pt_ps, 1)

                def values(k, j):
                    pe.wait_ge(pt_ready, 4 * k + j + 1)
                    for c in range(2):
                        for e in range(2):
                            h = 2 * j + e
                            mm = pe.matmul(bank[e * DH:(e + 1) * DH, 7, j * P:(j + 1) * P], v_sb[:, c, h * DH:(h + 1) * DH],
                                           pT[:, j % 2, (e * 2 + c) * P:(e * 2 + c + 1) * P], start=(c == 0), stop=(c == 1))
                    mm.then_inc(pv_done, 1)

                f0 = lay * (NB + 1)
                transposes(f0 + lay)
                for s in range(6):
                    project(f0, s)
                transposes(f0 + lay + 1)
                turn_qk(f0, 0)
                turn_qk(f0, 1)
                pe.wait_ge(kT_ready, f0 + 1)
                pe.wait_ge(q_even, f0 + 1)
                pe.wait_ge(q_odd, f0 + 1)
                pe.wait_ge(wo_loaded, 16 * 8 * (lay + 1))
                scores(lay * NB, 0)
                with pe.Fori(0, NB // 2) as u:
                    for i in range(2):
                        k = lay * NB + u * 2 + i
                        f = f0 + u * 2 + i + 1
                        scores(k, 1)
                        project(f, 0)
                        project(f, 1)
                        scores(k, 2)
                        project(f, 2)
                        project(f, 3)
                        scores(k, 3)
                        turn_probs(k, 0)
                        turn_probs(k, 1)
                        values(k, 0)
                        project(f, 4)
                        values(k, 1)
                        turn_probs(k, 2)
                        turn_probs(k, 3)
                        project(f, 5)
                        values(k, 2)
                        transposes(f + lay + 1)
                        values(k, 3)
                        turn_qk(f, 0)
                        turn_qk(f, 1)
                        pe.wait_ge(ot_ready, k + 1)
                        project_out(k, 0)
                        project_out(k, 1)
                        project_out(k, 2)
                        pe.wait_ge(kT_ready, f + 1)
                        pe.wait_ge(q_even, f + 1)
                        pe.wait_ge(q_odd, f + 1)
                        scores(k + 1, 0)
                        project_out(k, 3)
                end_phase(pe, 5 + 4 * lay)
                def turn_norm(n):
                    pe.wait_ge(n_norm, 8 * (n + 1))
                    for c in range(DC):
                        for i in range(GB):
                            tr = pe.transpose(bank[:, 6 + c, i * P:(i + 1) * P], hn[:, i, c * P:(c + 1) * P], ident[:])
                    tr.then_inc(nT_ps, 1)

                def up(k, j, half):
                    w = fw(j)
                    if j >= 2:
                        pe.wait_ge(g_ready, FC * k + j - 1)
                    for to, first, done in ((0, HID, g_ps), (2, 0, a_ps)):
                        if to == 2 and j >= 2:
                            pe.wait_ge(act_ready, FC * k + j - 1)
                        cols = slice(first + j * FW, first + j * FW + w)
                        for c in range(DC):
                            pe.matmul(bank[0:w, to + j % 2], w1_hi[:, c, cols], h_hi[:, half, c], start=(c == 0), stop=False)
                            pe.matmul(bank[0:w, to + j % 2], w1_lo[:, c, cols], h_hi[:, half, c], start=False, stop=False)
                            mm = pe.matmul(bank[0:w, to + j % 2], w1_hi[:, c, cols], h_lo[:, half, c], start=False, stop=(c == DC - 1))
                        mm.then_inc(done, 1)

                def down(k, j):
                    w = fw(j)
                    pe.wait_ge(act_lo_ready, FC * k + j + 1)
                    if j == 0:
                        pe.wait_ge(x_ffn, 1 + 2 * k)
                    for i in range(GB):
                        to = bank[:, 4 + i // 2, (i % 2) * D:(i % 2 + 1) * D]
                        tok = slice(i * P, (i + 1) * P)
                        pe.matmul(to, act_hi[0:w, j % 3, tok], w2_hi[0:w, j], start=(j == 0 and i % 2 == 0), stop=False, skip_group_check=True)
                        pe.matmul(to, act_hi[0:w, j % 3, tok], w2_lo[0:w, j], start=False, stop=False, skip_group_check=True)
                        mm = pe.matmul(to, act_lo[0:w, j % 3, tok], w2_hi[0:w, j], start=False, stop=(j == FC - 1), skip_group_check=True)
                    mm.then_inc(w2_used, 1)

                n0 = lay * (NG + 1)
                turn_norm(n0)
                end_phase(pe, 6 + 4 * lay)
                with pe.Fori(0, NG // 2) as u:
                    for i in range(2):
                        k = lay * NG + u * 2 + i
                        n = n0 + u * 2 + i
                        pe.wait_ge(nT_lo, 1 + 2 * n + 2)
                        for j in range(FC + 2):
                            if j < FC:
                                up(k, j, i)
                            if j >= 2:
                                down(k, j - 2)
                            if j == 3:
                                turn_norm(n + 1)
                end_phase(pe, 7 + 4 * lay)

        @block.vector
        def _(dve):
            dve.wait_ge(consts_ready, 1)
            def x_moments(u, i):
                g = u * 2 + i
                dve.wait_ge(x_loaded[i], 16 * (u + 1))
                settle(dve)
                for b in range(GB):
                    dve.bn_stats(l_bst[:, i, b], x_in[:, i, b]).then_inc(l_stat_step, 1)
                dve.wait_ge(l_stat_step, (g + 1) * GB)
                settle(dve)
                for b in range(GB):
                    dve.bn_aggr(l_mv[:, i, b], l_bst[:, i, b]).then_inc(l_stats, 1)

            def x_norm(g, i):
                dve.wait_ge(l_rs, g + 1)
                if type(g) is not int or g:
                    dve.wait_ge(xnT_ps, 1 + 2 * g)
                    dve.wait_ge(l_copied, 1 + g)
                for b in range(GB):
                    dve.tensor_scalar(xn_st[:, b], x_in[:, i, b], l_mv[:, i, b, 0:1], l_rstd[:, i, b:b + 1],
                                      ALU.subtract, ALU.mult).then_inc(l_norm, 1)
                dve.wait_ge(l_norm, (g + 1) * GB)
                dve.tensor_copy(x_sb[:, bass.ds(g * GB, GB), :], xn_st[:]).then_inc(l_copied, 1)

            x_moments(0, 0)
            with dve.Fori(0, NG // 2 - 1) as u:
                x_moments(u, 1)
                x_norm(u * 2, 0)
                x_moments(u + 1, 0)
                x_norm(u * 2 + 1, 1)
            x_moments(NG // 2 - 1, 1)
            x_norm(NG - 2, 0)
            x_norm(NG - 1, 1)
            end_phase(dve, 1)

            dve.wait_ge(row_t_ps, 1)
            dve.tensor_copy(turned, bank[:, 6:8].rearrange("p a (c n) -> p (a c) n", n=64)).then_inc(row_t_ready, 1)
            dve.tensor_copy(left[:], rows[:]).then_inc(topk_step, 1)
            dve.wait_ge(gate_exp, 3)
            dve.tensor_scalar(gate[:], gate[:], 1.0, None, ALU.add).then_inc(gate_step, 1)
            dve.wait_ge(gate_step, 1)
            dve.reciprocal(gate[:], gate[:]).then_inc(gate_step, 1)
            dve.wait_ge(gate_step, 2)
            dve.tensor_reduce(gsum[:], gate[:], AX_X, ALU.add).then_inc(gate_step, 1)
            dve.wait_ge(gate_step, 3)
            dve.tensor_scalar(gsum[:], gsum[:], 1e-6, None, ALU.add).then_inc(gate_step, 1)
            dve.wait_ge(gate_step, 4)
            dve.reciprocal(gsum[:], gsum[:]).then_inc(gate_step, 1)
            dve.wait_ge(gate_step, 5)
            dve.tensor_tensor(gate[:], gate[:], gsum[:, :, :, None].broadcast_to([P, BPB, B, 3]), ALU.mult).then_inc(gate_step, 1)
            dve.wait_ge(gate_step, 6)
            dve.wait_ge(w_loaded, 16 * NLOAD)

            def topk_round(r):
                dve.wait_ge(topk_step, 2 * r + 1)
                dve.max(top8[:], left[:]).then_inc(topk_step, 1)
                dve.wait_ge(topk_step, 2 * r + 2)
                dve.match_replace(left[:], top8[:], left[:], MARK).then_inc(topk_step, 1)

            rounds = 0
            for job, (T, b, at, n0) in enumerate(JOBS):
                if T == NCOMP:
                    for _ in range(5):
                        topk_round(rounds)
                        rounds += 1
                elif b == 0:
                    while rounds < ROUNDS:
                        topk_round(rounds)
                        rounds += 1
                    dve.wait_ge(topk_step, 2 * ROUNDS + 1)
                    dve.tensor_scalar(left[:], left[:], MARK, None, ALU.is_equal).then_inc(topk_step, 1)
                    dve.wait_ge(topk_step, 2 * ROUNDS + 2)
                    dve.tensor_tensor_scan(place_row[:], left[:], left[:], 0.0, ALU.add, ALU.max).then_inc(topk_step, 1)
                    dve.wait_ge(topk_step, 2 * ROUNDS + 3)
                    dve.tensor_tensor(place_row[:], place_row[:], left[:], ALU.mult).then_inc(topk_step, 1)
                    dve.wait_ge(pos_ps, 1)
                    dve.tensor_copy(turned, bank[:, 6:8].rearrange("p a (c n) -> p (a c) n", n=64)).then_inc(pos_ready, 1)
                    dve.wait_ge(pos_ready, 1)
                if T != NCOMP:
                    for c in range(BPB):
                        n = b * BPB + c
                        if n >= 2:
                            dve.wait_ge(sel_used, n - 1)
                        dve.tensor_scalar(sel_m[:, n % 2], iota1[:], turned[:, c, 32 * b:32 * b + 1], None, ALU.is_equal).then_inc(sel_made, 1)
                dve.wait_ge(com_v_ps, job + 1)
                dve.tensor_tensor(vc[:, 0:T // P], bank[:, 0:2].rearrange("p a (k d) -> p (a k) d", d=D)[:, 0:T // P],
                                  bv_bc[:, None, :].broadcast_to([P, T // P, D]), ALU.add).then_inc(com_v, 1)
                for qb in range(T // P):
                    n = n0 + qb
                    if T == NCOMP and rounds < ROUNDS - 1:
                        topk_round(rounds)
                        rounds += 1
                    dve.wait_ge(com_s, n + 1)
                    dve.tensor_reduce(c_max[:, 0:1], bank[:, 6, 0:T], AX_X, ALU.max).then_inc(com_m, 1)
                    dve.wait_ge(com_m, n + 1)
                    dve.tensor_scalar(c_max[:, 1:2], c_max[:, 0:1], -SCALE, None, ALU.mult).then_inc(com_nm, 1)
                    dve.wait_ge(com_e, n + 1)
                    dve.reciprocal(c_max[:, 3:4], c_max[:, 2:3]).then_inc(com_f, 1)
                    dve.wait_ge(com_f, 2 * n + 1)
                    which = 0 if T == NCOMP else 1
                    dve.tensor_tensor(c_max[:, 3:4], c_max[:, 3:4], gate[:, qb, b, which:which + 1], ALU.mult).then_inc(com_f, 1)
                    dve.wait_ge(com_f, 2 * n + 2)
                    dve.tensor_scalar(pc[:, 0:T], pc[:, 0:T], c_max[:, 3:4], None, ALU.mult).then_inc(com_p, 1)
            for n in range(B * (NCOMP // P)):
                b, qb = divmod(n, NCOMP // P)
                dve.wait_ge(com_o, n + 1)
                dve.wait_ge(bo_added, b + 1)
                dve.tensor_tensor(x_sb[:, b * BPB + qb], bank[:, 6, 0:D], x_sb[:, b * BPB + qb], ALU.add).then_inc(com_add, 1)
            end_phase(dve, 2)

            def win_values(j):
                dve.wait_ge(win_v_ps, j + 1)
                if type(j) is not int or j:
                    dve.wait_ge(win_c_ps, j)
                dve.tensor_tensor(vw[0:WK, :], bank[0:WK, 2, 0:D], bv_bc[0:WK, :], ALU.add).then_inc(win_v, 1)

            def win_hide(j):
                dve.wait_ge(win_s, j + 1)
                if type(j) is not int or j:
                    dve.wait_ge(win_pt_ps, j)
                settle(dve)
                dve.tensor_tensor_reduce(pw[:], bank[:, 3, 0:WK], mask_win[:], -SCALE, 3e38, ALU.add, ALU.min, w_max[:, 0:1]).then_inc(win_m, 1)

            def win_inverse(j):
                dve.wait_ge(win_e, j + 1)
                dve.reciprocal(w_max[:, 3:4], w_max[:, 2:3]).then_inc(win_f, 1)

            def win_weigh(j):
                dve.wait_ge(win_f, j + 1)
                dve.tensor_scalar(pw[:], pw[:], w_max[:, 3:4], gate[:, j % BPB, (j % NB) // BPB, 2:3], ALU.mult, ALU.mult).then_inc(win_p, 1)

            def win_add_up(j):
                dve.wait_ge(win_o, j + 1)
                dve.tensor_tensor(x_sb[:, j, :], bank[:, 6, 0:D], x_sb[:, j, :], ALU.add).then_inc(win_add, 1)

            def sum_stats(b):
                dve.wait_ge(win_add, 1 + b + 1)
                settle(dve)
                dve.bn_stats(m_bst[:], x_sb[:, b, :]).then_inc(m_stats, 1)

            def sum_moments(b):
                dve.wait_ge(m_stats, b + 1)
                settle(dve)
                dve.bn_aggr(m_mv[:], m_bst[:]).then_inc(m_aggr, 1)

            def norm_sum(b):
                dve.wait_ge(m_scaled, b + 1)
                dve.tensor_scalar(xn_st[:, 0], x_sb[:, b, :], m_mv[:, 0:1], m_scale[:], ALU.subtract, ALU.mult).then_inc(m_norm, 1)

            def make_x1(b):
                dve.wait_ge(m_norm, b + 1)
                dve.wait_ge(x0_loaded, 16 * (b // GB + 1))
                dve.tensor_tensor(x0_in[:, b % (2 * GB), :], x0_in[:, b % (2 * GB), :], xn_st[:, 0], ALU.add).then_inc(x1_made, 1)

            def x1_moments(b):
                dve.wait_ge(x1_made, b + 1)
                settle(dve)
                dve.bn_stats(f_bst1[:], x0_in[:, b % (2 * GB), :]).then_inc(x1_stats, 1)

            def x1_aggregate(b):
                dve.wait_ge(x1_stats, b + 1)
                settle(dve)
                dve.bn_aggr(f_mv1[:], f_bst1[:]).then_inc(x1_aggr, 1)

            def norm_x1(b):
                dve.wait_ge(x1_root, b + 1)
                dve.tensor_scalar(x_sb[:, b, :], x0_in[:, b % (2 * GB), :], f_mv1[:, 0:1], f_r[:], ALU.subtract, ALU.mult).then_inc(x_made, 1)

            def window_step(j, before):
                win_values(j + 1)
                win_hide(j + 1)
                if before >= 2:
                    x1_moments(j - 2)
                win_inverse(j + 1)
                if before >= 2:
                    x1_aggregate(j - 2)
                win_weigh(j + 1)
                win_add_up(j)
                if before >= 1:
                    norm_sum(j - 1)
                sum_stats(j)
                if before >= 1:
                    make_x1(j - 1)
                sum_moments(j)
                if before >= 2:
                    norm_x1(j - 2)

            win_values(0)
            win_hide(0)
            win_inverse(0)
            win_weigh(0)
            window_step(0, 0)
            window_step(1, 1)
            with dve.Fori(2, NB) as j:
                window_step(j, 2)
            arrive(dve)
            x1_moments(NB - 2)
            x1_aggregate(NB - 2)
            norm_sum(NB - 1)
            make_x1(NB - 1)
            norm_x1(NB - 2)
            x1_moments(NB - 1)
            x1_aggregate(NB - 1)
            norm_x1(NB - 1)
            dve.wait_ge(x_made, NB)
            await_phase(dve, 3)

            for c in range(DC):
                dve.wait_ge(split_hi, c + 1)
                dve.tensor_tensor(wqkv_lo[:, c], raw[:, c], wqkv_hi[:, c], ALU.subtract)

            with dve.Fori(0, DEPTH) as lay:
                dve.wait_ge(sc_made, 18 + 6 * (lay + 1))
                cs = raw[:, 2, 0:BPB * 64].rearrange("p (t k d) -> p t k d", t=BPB, k=2)
                for i in range(2):
                    for h in range(2):
                        dve.tensor_tensor(rope[:, :, 0, i, 32 * h:32 * h + 32], cs[:, :, i, :],
                                          sc_x[:, 0, i, 32 * h:32 * h + 32][:, None, :].broadcast_to([P, BPB, 32]), ALU.mult)
                sn = pT[:].rearrange("p a (t k d) -> p (a t) k d", k=2, d=32)
                dve.tensor_tensor(rope[:, :, 1, 1, 32:64], sn[:, :, 1, :],
                                  sc_x[:, 1, 1, 32:64][:, None, :].broadcast_to([P, BPB, 32]), ALU.mult)
                end_phase(dve, 4 + 4 * lay)

                def lo(g):
                    dve.wait_ge(hT_hi_ready, g + 1)
                    dve.tensor_tensor(hT_lo[:], bank[:, 5, 0:2 * P].rearrange("p (c t) -> p c t", c=DC), hT_hi[:], ALU.subtract).then_inc(hT_lo_ready, 1)

                def cosines(f, t, which):
                    dve.wait_ge(squares[which], f + 1)
                    dve.tensor_tensor(qk_cos[:, which].rearrange("p (h d) -> p h d", d=DH), bank[:, which].rearrange("p (h d) -> p h d", d=DH),
                                      rope[:, t % BPB, 0, which][:, None, :].broadcast_to([P, HEADS, DH]), ALU.mult).then_inc(rotated[which], 1)

                def sines(t, which):
                    dve.tensor_tensor(qk_sin[:, which].rearrange("p (h a d) -> p h a d", a=2, d=DH // 2),
                                      bank[:, which].rearrange("p (h a d) -> p h a d", a=2, d=DH // 2)[:, :, ::-1, :],
                                      rope[:, t % BPB, 1, which].rearrange("p (a d) -> p a d", a=2)[:, None, :, :].broadcast_to([P, HEADS, 2, DH // 2]),
                                      ALU.mult).then_inc(rotated[which], 1)

                def sums(f, which):
                    dve.wait_ge(squares[which], f + 1)
                    dve.tensor_reduce(sumsq[:, which * HEADS:(which + 1) * HEADS], qk_sq[:, which].rearrange("p (h d) -> p h d", d=DH),
                                      AX_X, ALU.add).then_inc(ss_ready[which], 1)

                def floor_sums(f, which):
                    part = slice(which * HEADS, (which + 1) * HEADS)
                    dve.wait_ge(ss_ready[which], f + 1)
                    settle(dve)
                    dve.tensor_scalar(sumsq[:, part], sumsq[:, part], 1e-24, None, ALU.max).then_inc(ss_floor[which], 1)

                def add_k(f):
                    dve.wait_ge(rotated[1], 2 * f + 2)
                    dve.tensor_tensor(qk_cos[:, 1], qk_cos[:, 1], qk_sin[:, 1], ALU.add).then_inc(z_ready[1], 1)

                def normalise(f, which):
                    dve.wait_ge(r_ready[which], f + 1)
                    dve.wait_ge(z_ready[which], f + 1)
                    z = qk_cos[:, which].rearrange("p (h d) -> p h d", d=DH)
                    dve.tensor_tensor(z, z, rnorm[:, which * HEADS:(which + 1) * HEADS, None].broadcast_to([P, HEADS, DH]), ALU.mult).then_inc(qk_ready[which], 1)

                def k_out(f, half):
                    dve.wait_ge(qkT_ps[1], f + 1)
                    dve.tensor_copy(kT[:, :, half], bank[:, 1].rearrange("p (c t) -> p c t", t=P)).then_inc(kT_ready, 1)

                def q_even_out(f):
                    dve.wait_ge(qkT_ps[0], f + 1)
                    dve.tensor_copy(qT[0:DH, :, 0], bank[0:DH, 0].rearrange("p (c t) -> p c t", t=P)).then_inc(q_even, 1)

                f0 = lay * (NB + 1)

                def hide(i, k, h):
                    mask = (mask_even, mask_odd)[i]
                    dve.wait_ge(s_ready, 4 * k + lay + h // 2 + 1)
                    settle(dve)
                    dve.tensor_tensor_reduce(prob[:, h].rearrange("p a b -> p (a b)"), bank[:, 3 + (h // 2) % 2, (h % 2) * 2 * P:(h % 2 + 1) * 2 * P],
                                             mask[:].rearrange("p a b -> p (a b)"), 1.0, 3e38, ALU.add, ALU.min, neg_max[:, h:h + 1]).then_inc(masked, 1)

                lo(f0 + lay)
                for which in range(2):
                    sums(f0, which)
                    floor_sums(f0, which)
                    cosines(f0, 0, which)
                    sines(0, which)
                lo(f0 + lay + 1)
                add_k(f0)
                normalise(f0, 0)
                normalise(f0, 1)
                q_even_out(f0)
                k_out(f0, 0)
                dve.wait_ge(mask_set, lay * (NB // 2 + 1) + 1)
                hide(0, lay * NB, 0)
                hide(0, lay * NB, 1)
                with dve.Fori(0, NB // 2) as u:
                    for i in range(2):
                        t = u * 2 + i
                        k = lay * NB + t
                        f = f0 + t + 1
                        def weigh(h):
                            for e in range(2):
                                dve.wait_ge(exped, HEADS * k + h + e + 1)
                                dve.reciprocal(pinv[:, h + e:h + e + 1], psums[:, h + e:h + e + 1]).then_inc(inverted, 1)
                            dve.wait_ge(inverted, HEADS * k + h + 1)
                            dve.tensor_scalar(prob[:, h], prob[:, h], pinv[:, h:h + 1], None, ALU.mult).then_inc(p_even, 1)

                        hide(i, k, 2)
                        hide(i, k, 3)
                        weigh(0)
                        weigh(2)
                        hide(i, k, 4)
                        hide(i, k, 5)
                        sums(f, 0)
                        cosines(f, t + 1, 0)
                        floor_sums(f, 0)
                        hide(i, k, 6)
                        hide(i, k, 7)
                        sines(t + 1, 0)
                        sums(f, 1)
                        weigh(4)
                        weigh(6)
                        floor_sums(f, 1)
                        cosines(f, t + 1, 1)
                        sines(t + 1, 1)
                        add_k(f)
                        normalise(f, 0)
                        normalise(f, 1)
                        q_even_out(f)
                        k_out(f, 1 - i)
                        lo(f + lay + 1)
                        if i == 1:
                            dve.wait_ge(mask_set, lay * (NB // 2 + 1) + u + 2)
                        hide(1 - i, k + 1, 0)
                        hide(1 - i, k + 1, 1)
                        dve.wait_ge(wo_ps, k + 1)
                        dve.tensor_tensor(x_sb[:, t, :], bank[:, 6, 0:D], x_sb[:, t, :], ALU.add).then_inc(x_attn, 1)
                end_phase(dve, 5 + 4 * lay)

                def norm_stats(n, g):
                    for b in range(GB):
                        t = g * GB + b
                        dve.bn_stats(bst[:, b, 0], x_sb[:, t, 0:P]).then_inc(n_stats, 1)
                        dve.bn_stats(bst[:, b, 1], hs_ffn[:, t + t // BPB, :]).then_inc(n_stats, 1)
                    dve.wait_ge(n_stats, 2 * GB * (n + 1))
                    settle(dve)
                    for b in range(GB):
                        dve.bn_aggr(mv[:, b], bst[:, b].rearrange("p a s -> p (a s)")).then_inc(n_aggr, 1)

                def norm_apply(n, g):
                    dve.wait_ge(n_rs, n + 1)
                    dve.wait_ge(nT_ps, 1 + n)
                    settle(dve)
                    for b in range(GB):
                        t = g * GB + b
                        for c, src in enumerate((x_sb[:, t, 0:P], hs_ffn[:, t + t // BPB, :])):
                            dve.tensor_scalar(hn[:, b, c * P:(c + 1) * P], src, mv[:, b, 0:1], rstd[:, b:b + 1],
                                              ALU.subtract, ALU.mult).then_inc(n_norm, 1)

                def norm_full(n):
                    dve.wait_ge(nT_lo, 1 + 2 * n)
                    for c in range(DC):
                        dve.wait_ge(nT_hi, 2 * n + c + 1)
                        dve.tensor_scalar(h_full[:, c], bank[:, 6 + c], ln_gb[:, 0, c:c + 1], ln_gb[:, 1, c:c + 1], ALU.mult, ALU.add).then_inc(nT_full, 1)

                n0 = lay * (NG + 1)
                dve.wait_ge(wo_loaded, 16 * 8 * (lay + 1))
                dve.wait_ge(split_hi, SPLITS * lay + DC + 1)
                dve.tensor_tensor(w1_lo[:, 0], raw[:, 0, 0:2 * HID], w1_hi[:, 0], ALU.subtract)
                dve.wait_ge(hs_ffn_moved, 32 * (NB * lay + GB))
                settle(dve)
                norm_stats(n0, 0)
                norm_apply(n0, 0)
                raw_w2 = raw[:, 2, :].rearrange("p (c n) -> p c n", n=D)
                dve.wait_ge(split_hi, SPLITS * lay + DC + 4)
                dve.tensor_tensor(w2_lo[0:FW, 0:FC - 1], raw_w2[0:FW, 0:FC - 1], w2_hi[0:FW, 0:FC - 1], ALU.subtract)
                dve.tensor_tensor(w2_lo[0:fw(FC - 1), FC - 1], raw_w2[0:fw(FC - 1), FC - 1], w2_hi[0:fw(FC - 1), FC - 1], ALU.subtract)
                norm_full(n0)
                end_phase(dve, 6 + 4 * lay)
                with dve.Fori(0, NG // 2) as u:
                    for i in range(2):
                        g = u * 2 + i
                        k = lay * NG + g
                        n = n0 + g + 1
                        for j in range(FC):
                            w = fw(j)
                            dve.wait_ge(a_ps, FC * k + j + 1)
                            dve.wait_ge(g_ready, FC * k + j + 1)
                            if j >= 2:
                                dve.wait_ge(act_lo_ready, FC * k + j - 1)
                            dve.scalar_tensor_tensor(out=act_full[0:w, j % 2], in0=bank[0:w, 2 + j % 2], scalar=b1_sb[0:w, 0, j:j + 1],
                                                     in1=gelu_sb[0:w, j % 2], op0=ALU.add, op1=ALU.mult).then_inc(act_ready, 1)
                            if j >= 3:
                                dve.wait_ge(w2_used, FC * k + j - 2)
                            dve.wait_ge(act_ready, FC * k + j + 1)
                            dve.tensor_copy(act_hi[0:w, j % 3], act_full[0:w, j % 2]).then_inc(act_hi_ready, 1)
                            if j == 0:
                                norm_stats(n, (g + 1) % NG)
                            if j == 2:
                                norm_apply(n, (g + 1) % NG)
                            if j == 4:
                                norm_full(n)
                        if i == 1:
                            dve.wait_ge(split_hi, SPLITS * lay + DC + 4 + u + 1)
                            dve.tensor_tensor(wqkv_lo[:, :, bass.ds(u * SHARE, SHARE)], raw[:, 0:2, bass.ds(u * SHARE, SHARE)],
                                              wqkv_hi[:, :, bass.ds(u * SHARE, SHARE)], ALU.subtract)
                        dve.wait_ge(w2_used, FC * (k + 1))
                        dve.wait_ge(b2_added, k + 1)
                        for h in range(2):
                            xs = x_sb[:, bass.ds(g * GB + 2 * h, 2), :]
                            dve.tensor_tensor(xs, bank[:, 4 + h].rearrange("p (b d) -> p b d", d=D), xs, ALU.add).then_inc(x_ffn, 1)
                end_phase(dve, 7 + 4 * lay)

            def last_moments(g, i):
                for b in range(GB):
                    dve.bn_stats(f_bst[:, i, b], x_sb[:, g * GB + b, :]).then_inc(f_step, 1)
                dve.wait_ge(f_step, (g + 1) * GB)
                settle(dve)
                for b in range(GB):
                    dve.bn_aggr(f_mv[:, i, b], f_bst[:, i, b]).then_inc(f_stats, 1)

            def last_norm(u, i):
                g = u * 2 + i
                dve.wait_ge(f_rs, g + 1)
                if type(u) is not int or u:
                    dve.wait_ge(out_stored[i], 1 + 16 * u)
                settle(dve)
                for b in range(GB):
                    dve.tensor_scalar(f_y[:, i, b], x_sb[:, g * GB + b, :], f_mv[:, i, b, 0:1], f_rstd[:, i, b:b + 1], ALU.subtract, ALU.mult).then_inc(f_norm, 1)

            last_moments(0, 0)
            with dve.Fori(0, NG // 2 - 1) as u:
                last_moments(u * 2 + 1, 1)
                last_norm(u, 0)
                last_moments(u * 2 + 2, 0)
                last_norm(u, 1)
            last_moments(NG - 1, 1)
            last_norm(NG // 2 - 1, 0)
            last_norm(NG // 2 - 1, 1)


_INS = ["L0_attn_hidden_states", "L0_attn_Wq", "L0_attn_bq", "L0_attn_Wk", "L0_attn_bk", "L0_attn_Wv", "L0_attn_bv", "L0_attn_Wo",
        "L0_attn_bo", "L0_attn_Wg", "L0_attn_bg", "L0_attn_Wc", "L0_attn_bc", "L0_attn_Ws", "L0_attn_bs", "L0_ffn_wqkv",
        "L0_ffn_q_scale", "L0_ffn_k_scale", "L0_ffn_wo", "L0_ffn_ln_g", "L0_ffn_ln_b", "L0_ffn_w1", "L0_ffn_b1", "L0_ffn_w2", "L0_ffn_b2"]


def rope_constants():
    half = np.arange(0, DH, 2, dtype=np.float32)
    inv_freq = (1.0 / 10000.0 ** (half / DH)).astype(np.float32)
    t = np.arange(N, dtype=np.float32)
    freqs = (t[:, None] * inv_freq[None, :]).astype(np.float32).astype(np.float64)
    base = (half + 0.4 * DH).astype(np.float64) / (1.4 * DH)
    scale = base[None, :] ** (((t - N // 2) / 64.0).astype(np.float64))[:, None]
    tab = np.stack([np.stack([f(freqs) * scale, f(freqs) / scale], 1) for f in (np.cos, np.sin)])
    tab = tab.reshape(2, BPB, P, 2, DH // 2).transpose(2, 0, 1, 3, 4)
    return np.ascontiguousarray(tab.reshape(P, 2, BPB * 64)).astype(np.float32)


def kernel(**inputs):
    import concourse.bacc as _bacc
    from concourse.bass_utils import run_bass_kernel_spmd as _run

    nc = _bacc.Bacc("TRN2", target_bir_lowering=False, num_devices=1)
    arrays, args = {}, []
    for name in _INS:
        a = np.ascontiguousarray(inputs[name])
        arrays[f"in_{name}"] = a
        args.append(nc.dram_tensor(f"in_{name}", a.shape, mybir.dt.from_np(a.dtype), kind="ExternalInput").ap())
    arrays["rope_base"] = rope_constants()
    args.append(nc.dram_tensor("rope_base", arrays["rope_base"].shape, F32, kind="ExternalInput").ap())
    args.append(nc.dram_tensor("out", (B, N, D), F32, kind="ExternalOutput").ap())
    build(nc, *args)
    r = _run(nc, [arrays], core_ids=[0])
    return r.results[0]["out"]
```
